# Optimizing a Trainium2 kernel written in Bass

```python
import numpy as np
import jax
import jax.numpy as jnp

def _softmax(x, axis=-1):
    return jax.nn.softmax(x, axis=axis)

def _gelu(x):
    return jax.nn.gelu(x, approximate=True)

def _silu(x):
    return jax.nn.silu(x)

def _sigmoid(x):
    return jax.nn.sigmoid(x)

def _layernorm(x, axis=-1, eps=1e-05):
    m = jnp.mean(x, axis=axis, keepdims=True)
    v = jnp.var(x, axis=axis, keepdims=True)
    return (x - m) / jnp.sqrt(v + eps)

def _scatter_add(tgt, idx, src, axis=0):
    return tgt.at[idx].add(src)

def _segment_sum(src, seg, n):
    return jax.ops.segment_sum(src, seg, n)
kernel_name = 'mk_decoder_postln_d1_seqx_r8_822bce'

def setup_inputs(seed: int=0):
    np.random.seed(seed)
    _w = jnp.asarray

    def _rec_inputs():
        import jax
        import jax.numpy as jnp
        _rk = jax.random.key(seed)
        x = 7.22e-05 + 1 * jax.random.normal(jax.random.fold_in(_rk, 1), (4, 256, 256), jnp.float32)
        _lenS = 256 - jax.random.randint(jax.random.fold_in(_rk, 7), (4,), 0, max(1, 256 // 4) + 1, jnp.int32)
        _lenS2 = 256 - jax.random.randint(jax.random.fold_in(_rk, 8), (4,), 0, max(1, 256 // 4) + 1, jnp.int32)
        _ctx_1024P = jax.random.normal(jax.random.fold_in(_rk, 11), (4, 16, 128), jnp.float32)
        _ctx_1024c = jax.random.dirichlet(jax.random.fold_in(_rk, 511), 0.3 * jnp.ones((16,), jnp.float32), (4, 256))
        _ctx_1024t = jnp.einsum('bsk,bkd->bsd', _ctx_1024c, _ctx_1024P)
        _ctx_1024t = _ctx_1024t * jax.lax.rsqrt(jnp.mean(jnp.square(_ctx_1024t)) + 1e-12) * 0.953939
        ctx_1024 = 2.81802e-05 + 1.00001 * (_ctx_1024t + 0.3 * jax.random.normal(jax.random.fold_in(_rk, 611), (4, 256, 128), jnp.float32))
        return (x, ctx_1024)
    x, ctx_1024 = _rec_inputs()

    def _L0_attn_setup():
        import math
        import jax, jax.numpy as jnp
        import numpy as np
        B, T, D = (2, 256, 256)
        NH, NKV = (32, 8)
        HD = D // NH
        key = jax.random.key(seed)
        kx, kq, kk, kv, ko = jax.random.split(key, 5)
        s = 1.0 / math.sqrt(D)
        return {'x': jax.random.normal(kx, (B, T, D), dtype=jnp.float32), 'wq': jax.random.normal(kq, (D, NH * HD), dtype=jnp.float32) * s, 'wk': jax.random.normal(kk, (D, NKV * HD), dtype=jnp.float32) * s, 'wv': jax.random.normal(kv, (D, NKV * HD), dtype=jnp.float32) * s, 'wo': jax.random.normal(ko, (NH * HD, D), dtype=jnp.float32) * s}
    _L0_attn_all = _L0_attn_setup()
    _L0_attn_in = {k: v for k, v in _L0_attn_all.items() if k in ('wq', 'wk', 'wv', 'wo')}
    del _L0_attn_all

    def _L0_xattn_setup():
        import jax, jax.numpy as jnp
        import numpy as np
        key = jax.random.key(seed)
        ks = jax.random.split(key, 6)
        B, L, N, C, D = (8, 64, 256, 128, 128)
        return {'teacher_logits': jax.random.normal(ks[0], (B, L, N), dtype=jnp.float32), 'teacher_features': jax.random.normal(ks[1], (B, N, C), dtype=jnp.float32), 'Wq': jax.random.normal(ks[2], (D, C), dtype=jnp.float32) * (1.0 / np.sqrt(C)), 'bq': jnp.zeros((D,), dtype=jnp.float32), 'Wk': jax.random.normal(ks[3], (D, C), dtype=jnp.float32) * (1.0 / np.sqrt(C)), 'bk': jnp.zeros((D,), dtype=jnp.float32)}
    _L0_xattn_all = _L0_xattn_setup()
    _L0_xattn_in = {k: v for k, v in _L0_xattn_all.items() if k in ('Wq', 'bq', 'Wk', 'bk')}
    del _L0_xattn_all

    def _L0_ffn_setup():
        import jax, jax.numpy as jnp
        import numpy as np
        D = 256
        F = 176
        E = 8
        K = 2
        FS = 352
        B, S = (2, 128)
        key = jax.random.key(seed)
        ks = jax.random.split(key, 9)
        sc = 0.02
        return {'x': jax.random.normal(ks[0], (B, S, D), dtype=jnp.float32), 'Wr': jax.random.normal(ks[1], (E, D), dtype=jnp.float32) * sc, 'Wg': jax.random.normal(ks[2], (E, F, D), dtype=jnp.float32) * sc, 'Wu': jax.random.normal(ks[3], (E, F, D), dtype=jnp.float32) * sc, 'Wd': jax.random.normal(ks[4], (E, D, F), dtype=jnp.float32) * sc, 'Wsg': jax.random.normal(ks[5], (FS, D), dtype=jnp.float32) * sc, 'Wsu': jax.random.normal(ks[6], (FS, D), dtype=jnp.float32) * sc, 'Wsd': jax.random.normal(ks[7], (D, FS), dtype=jnp.float32) * sc}
    _L0_ffn_all = _L0_ffn_setup()
    _L0_ffn_in = {k: v for k, v in _L0_ffn_all.items() if k in ('Wr', 'Wg', 'Wu', 'Wd', 'Wsg', 'Wsu', 'Wsd')}
    del _L0_ffn_all
    return {'x': x, 'ctx_1024': ctx_1024, 'L0_attn_wq': _L0_attn_in['wq'], 'L0_attn_wk': _L0_attn_in['wk'], 'L0_attn_wv': _L0_attn_in['wv'], 'L0_attn_wo': _L0_attn_in['wo'], 'L0_xattn_Wq': _L0_xattn_in['Wq'], 'L0_xattn_bq': _L0_xattn_in['bq'], 'L0_xattn_Wk': _L0_xattn_in['Wk'], 'L0_xattn_bk': _L0_xattn_in['bk'], 'L0_ffn_Wr': _L0_ffn_in['Wr'], 'L0_ffn_Wg': _L0_ffn_in['Wg'], 'L0_ffn_Wu': _L0_ffn_in['Wu'], 'L0_ffn_Wd': _L0_ffn_in['Wd'], 'L0_ffn_Wsg': _L0_ffn_in['Wsg'], 'L0_ffn_Wsu': _L0_ffn_in['Wsu'], 'L0_ffn_Wsd': _L0_ffn_in['Wsd']}

def reference(x, ctx_1024, L0_attn_wq, L0_attn_wk, L0_attn_wv, L0_attn_wo, L0_xattn_Wq, L0_xattn_bq, L0_xattn_Wk, L0_xattn_bk, L0_ffn_Wr, L0_ffn_Wg, L0_ffn_Wu, L0_ffn_Wd, L0_ffn_Wsg, L0_ffn_Wsu, L0_ffn_Wsd):
    import jax
    import jax.numpy as jnp

    def _L0_attn_ref(x, wq, wk, wv, wo):
        import math
        import jax, jax.numpy as jnp
        import numpy as np
        B, T, D = (2, 256, 256)
        NH, NKV = (32, 8)
        HD = D // NH
        bsz, seqlen, _ = x.shape
        q = (x @ wq).reshape(bsz, seqlen, NH, HD).transpose(0, 2, 1, 3)
        k = (x @ wk).reshape(bsz, seqlen, NKV, HD).transpose(0, 2, 1, 3)
        v = (x @ wv).reshape(bsz, seqlen, NKV, HD).transpose(0, 2, 1, 3)
        rep = NH // NKV
        k = jnp.repeat(k, rep, axis=1)
        v = jnp.repeat(v, rep, axis=1)
        att = jnp.einsum('bhqd,bhkd->bhqk', q.astype(jnp.float32), k.astype(jnp.float32)) / math.sqrt(HD)
        mask = jnp.triu(jnp.ones((seqlen, seqlen), dtype=bool), k=1)
        att = jnp.where(mask[None, None, :, :], -jnp.inf, att)
        att = jax.nn.softmax(att, axis=-1)
        y = jnp.einsum('bhqk,bhkd->bhqd', att, v.astype(jnp.float32)).astype(q.dtype)
        y = y.transpose(0, 2, 1, 3).reshape(bsz, seqlen, NH * HD)
        return y @ wo

    def _L0_xattn_ref(teacher_logits, teacher_features, Wq, bq, Wk, bk):
        import jax, jax.numpy as jnp
        import numpy as np
        query = jnp.einsum('bnc,dc->bnd', teacher_features, Wq) + bq
        key = jnp.einsum('bnc,dc->bnd', teacher_features, Wk) + bk
        energy = jnp.einsum('bnd,bmd->bnm', query, key)
        attention = jax.nn.softmax(energy, axis=-1)
        x_m = jnp.einsum('bln,bmn->blm', teacher_logits, attention)
        return x_m

    def _L0_ffn_ref(x, Wr, Wg, Wu, Wd, Wsg, Wsu, Wsd):
        import jax, jax.numpy as jnp
        import numpy as np
        D = 256
        F = 176
        E = 8
        K = 2
        FS = 352
        B, S = (2, 128)
        silu = jax.nn.silu
        sg = silu(jnp.einsum('bsd,fd->bsf', x, Wsg))
        su = jnp.einsum('bsd,fd->bsf', x, Wsu)
        shared_out = jnp.einsum('bsf,df->bsd', sg * su, Wsd)
        logits = jnp.einsum('bsd,ed->bse', x, Wr)
        scores = jax.nn.softmax(logits, axis=-1)
        topk_scores, topk_idx = jax.lax.top_k(scores, K)
        w_full = jnp.sum(jax.nn.one_hot(topk_idx, E, dtype=x.dtype) * topk_scores[..., None], axis=-2)
        g = silu(jnp.einsum('bsd,efd->bsef', x, Wg))
        u = jnp.einsum('bsd,efd->bsef', x, Wu)
        out_e = jnp.einsum('bsef,edf->bsed', g * u, Wd)
        routed_out = jnp.einsum('bsed,bse->bsd', out_e, w_full)
        return routed_out + shared_out
    x = _layernorm(x + _L0_attn_ref(x, L0_attn_wq, L0_attn_wk, L0_attn_wv, L0_attn_wo), axis=-1)
    x = _layernorm(x + _L0_xattn_ref(x, ctx_1024, L0_xattn_Wq, L0_xattn_bq, L0_xattn_Wk, L0_xattn_bk), axis=-1)
    x = _layernorm(x + _L0_ffn_ref(x, L0_ffn_Wr, L0_ffn_Wg, L0_ffn_Wu, L0_ffn_Wd, L0_ffn_Wsg, L0_ffn_Wsu, L0_ffn_Wsd), axis=-1)
    return x

_drawn_inputs = setup_inputs


def setup_inputs(seed=0):
    import zlib

    import numpy as np

    out = dict(_drawn_inputs(seed))
    spreads = {'L0_xattn_bq': (0.0, 0.1), 'L0_xattn_bk': (0.0, 0.8)}
    factors = {'L0_ffn_Wr': 8.0,
     'L0_ffn_Wg': 8.0,
     'L0_ffn_Wu': 8.0,
     'L0_ffn_Wd': 8.0,
     'L0_ffn_Wsg': 2.884,
     'L0_ffn_Wsu': 2.86,
     'L0_ffn_Wsd': 2.863}
    for name, (base, spread) in spreads.items():
        noise = np.random.default_rng([zlib.crc32(name.encode()), seed]).standard_normal(out[name].shape)
        drawn = base * np.exp(spread * noise) if base else spread * noise
        out[name] = jnp.asarray(drawn.astype(out[name].dtype))
    for name, factor in factors.items():
        out[name] = (out[name] * factor).astype(out[name].dtype)
    return out
```

```python
from contextlib import ExitStack

import numpy as np

import concourse.bass as bass
from concourse import mybir

F32 = mybir.dt.float32
F32R = mybir.dt.float32r
BF16 = mybir.dt.bfloat16
ACT = mybir.ActivationFunctionType
ALU = mybir.AluOpType
AX_X = mybir.AxisListType.X

P = 128
B, T, D = 4, 256, 256
TC = T // P
DC = D // P
NH, NKV, HD = 32, 8, 8
REP = NH // NKV
CTX = 128
E, FE, FS = 8, 176, 352
PAIRS = E // 2 + 1
FP = 2 * FE
CH = [(0, 128), (128, 128), (256, 96)]
NCH = len(CH)
HALF = 512
NHALF = B * T // HALF
STEPS = PAIRS * NHALF * NCH
PSTEPS = NHALF * NCH
EPS = 1e-5
MASKED = -3e38
SCALE = float(HD) ** -0.5
COMBOS = [(0, 0), (0, 1), (1, 0), (1, 1), (0, 2), (2, 0)]
MROW = len(COMBOS) * HD
GUW = 2 * DC * FP
WW = GUW + NCH * D
NW = E + 1
RING = 6
SU = 24


def build_layer(nc, x_tok, x_T, ctx_T, w_qkv, w_o, xa_w, xa_b, w_r, w_ffn,
                c_ident, c_identb, c_mask, c_sel, c_lower, out):
    with ExitStack() as ctx:
        def sb(name, shape, dt=F32):
            return ctx.enter_context(nc.sbuf_tensor(name, shape, dt))

        def sem(name):
            return ctx.enter_context(nc.semaphore(name))

        ident = sb("ident", [P, P])
        identb = sb("identb", [P, P], BF16)
        mask = sb("mask", [P, REP, P], BF16)
        sel = sb("sel", [3 * NW, PAIRS * NCH * P], BF16)
        lower = sb("lower", [P, E, E])
        wqkv_s = sb("wqkv_s", [P, DC, NH * HD + 2 * NKV * HD])
        wo_s = sb("wo_s", [P, DC, D])
        xaw_s = sb("xaw_s", [P, 2, P])
        xab_s = sb("xab_s", [P, 2])
        wr_s = sb("wr_s", [P, DC, E])
        wr_hi = sb("wr_hi", [P, DC, E], F32R)
        wr_lo = sb("wr_lo", [P, DC, E], F32R)
        x_s = sb("x_s", [P, B * TC, D])
        xT_s = sb("xT_s", [P, 2, DC, T])
        ctxT_s = sb("ctxT_s", [P, 2, T])
        rest_q = sb("rest_q", [P, 2 * T])
        rest_k = sb("rest_k", [NKV * HD, T])
        part_q = sb("part_q", [P, 3, 2 * T], BF16)
        part_k = sb("part_k", [NKV * HD, 3, T], BF16)
        KTs = [sb(f"KTs{i}", [P, NKV, T], BF16) for i in range(2)]
        KTp = [sb(f"KTp{i}", [P, NKV, T], BF16) for i in range(2)]
        V = [sb(f"V{i}", [P, TC, NKV, 32]) for i in range(2)]
        negmax = sb("negmax", [P, TC, NH])
        rest_m = sb("rest_m", [P, TC, NH])
        ones = sb("ones", [3, NKV * T], BF16)
        part_m = sb("part_m", [P, TC, 3, NH], BF16)
        mrow = sb("mrow", [3 * NH, T], BF16)
        oT = sb("oT", [P, 2, TC, 512])
        rden = sb("rden", [P, REP * 4])
        y = sb("y", [P, TC, D])
        yT = sb("yT", [P, DC, T])
        res = sb("res", [P, TC, D])
        x1 = sb("x1", [P, TC, D])
        x1T = sb("x1T", [P, DC, T])
        stat = sb("stat", [P, TC, 6])
        mv = sb("mv", [P, TC, 2])
        veps = sb("veps", [P, TC])
        rstd = sb("rstd", [P, TC])
        mhalf = sb("mhalf", [P, TC])
        xaqk = sb("xaqk", [P, 2, T])
        xam = sb("xam", [P, TC])
        xae = sb("xae", [P, TC, T])
        xal = sb("xal", [P, TC])
        xar = sb("xar", [P, TC])
        attT = sb("attT", [P, TC, T])
        x2 = sb("x2", [P, B * TC, D])
        x2T_hi = sb("x2T_hi", [P, DC, B * T], F32R)
        x2T_lo = sb("x2T_lo", [P, DC, B * T], F32R)
        lmax = sb("lmax", [P, TC])
        lexp = sb("lexp", [P, TC, E])
        lsum = sb("lsum", [P, TC])
        score = sb("score", [P, TC, E])
        above = sb("above", [P, TC, E, E])
        equal = sb("equal", [P, TC, E, E])
        lsub = sb("lsub", [P, TC, E])
        rank = sb("rank", [P, TC, E])
        gatew = sb("gatew", [P, TC, NW])
        rest_g = sb("rest_g", [P, TC, NW])
        part_g = sb("part_g", [P, TC, 3, NW], BF16)
        gateT = sb("gateT", [3 * NW, B * T], BF16)
        w_in = sb("w_in", [P, WW])
        w_hi = [sb("w_hi0", [P, WW], F32R)]
        w_lo = [sb("w_lo0", [P, WW], F32R)]
        zero = sb("zero", [P, 512], BF16)
        with ExitStack() as attention:
            probs = attention.enter_context(nc.sbuf_tensor("probs", [P, RING, 3, 512], F32))
            QT = [attention.enter_context(nc.sbuf_tensor(f"QT{i}", [P, NH, T], BF16)) for i in range(2)]
        sg = [sb(f"sg{i}", [P, HALF]) for i in range(2)]
        gu = [sb(f"gu{i}", [P, HALF]) for i in range(2)]
        hid = [sb(f"hid{i}", [P, HALF]) for i in range(2)]
        h_hi = [sb(f"h_hi{i}", [P, HALF], F32R) for i in range(2)]
        h_lo = [sb(f"h_lo{i}", [P, HALF], F32R) for i in range(2)]
        w_hi.append(sb("w_hi1", [P, WW], F32R))
        w_lo.append(sb("w_lo1", [P, WW], F32R))

        bank = [ctx.enter_context(nc.psum_tensor(f"bank{i}", [P, 512], F32)) for i in range(8)]
        ST = bank[0:2]
        SQ = bank[2:4]
        PV = bank[4:6]
        M0, M1 = bank[6:8]
        G, U = [bank[4], M0], [bank[5], M1]
        M0b = M0[:, :].bitcast(BF16)

        ld = {n: sem(f"ld_{n}") for n in ("ident", "identb", "mask", "sel", "lower", "wqkv", "wo", "xaw", "xab",
                                          "wr", "x")}
        ld_xT = [sem(f"ld_xT{b}") for b in range(B)]
        ld_ctxT = [sem(f"ld_ctxT{b}") for b in range(B)]
        ones_rows = sem("ones_rows")
        ld_w = sem("ld_w")
        init_v = sem("init_v")
        init_p = sem("init_p")
        init_qt = sem("init_qt")
        wr_done = sem("wr_done")
        proj_done = sem("proj_done")
        hi_done = sem("hi_done")
        v_done = sem("v_done")
        parts_done = sem("parts_done")
        qk_rows = [sem(f"qk_rows{i}") for i in range(2)]
        sq_done = sem("sq_done")
        max_done = sem("max_done")
        mparts_done = sem("mparts_done")
        mT_done = sem("mT_done")
        mrow_done = sem("mrow_done")
        m_rows = sem("m_rows")
        st_done = sem("st_done")
        exp_done = sem("exp_done")
        causal_done = sem("causal_done")
        pv_done = sem("pv_done")
        oT_done = sem("oT_done")
        ot_done = sem("ot_done")
        y_done = sem("y_done")
        yt_done = sem("yt_done")
        yT_done = sem("yT_done")
        wo_done = sem("wo_done")
        res1_done = sem("res1_done")
        res2_done = sem("res2_done")
        x1_done = sem("x1_done")
        x1t_done = sem("x1t_done")
        x1T_done = sem("x1T_done")
        xm_done = sem("xm_done")
        x2_done = sem("x2_done")
        x2t_done = sem("x2t_done")
        x2hi_done = sem("x2hi_done")
        x2lo_done = sem("x2lo_done")
        var_done = sem("var_done")
        rstd_done = sem("rstd_done")
        xqk_done = sem("xqk_done")
        xqk_sb = sem("xqk_sb")
        xen_done = sem("xen_done")
        xmax_done = sem("xmax_done")
        xexp_done = sem("xexp_done")
        xatt_done = sem("xatt_done")
        xat_done = sem("xat_done")
        attT_done = sem("attT_done")
        lg_done = sem("lg_done")
        lsub_done = sem("lsub_done")
        lexp_done = sem("lexp_done")
        gparts_done = sem("gparts_done")
        gT_done = sem("gT_done")
        gateT_done = sem("gateT_done")
        dve = sem("dve")
        whi_done = sem("whi_done")
        wlo_done = sem("wlo_done")
        gu_done = sem("gu_done")
        silu_done = sem("silu_done")
        spread_done = sem("spread_done")
        prod_done = sem("prod_done")
        hid_done = sem("hid_done")
        hhi_done = sem("hhi_done")
        hlo_done = sem("hlo_done")
        down_done = sem("down_done")
        sums_done = sem("sums_done")
        rs_done = sem("rs_done")
        out_done = sem("out_done")
        stored = sem("stored")

        def schedule(proj, pre, mx, route, at, tail):
            proj(0)
            pre(0)
            proj(1)
            for u in range(SU):
                mx(0, u)
            route(0)
            for b in range(B):
                for u in range(SU):
                    at(b, u)
                    if b + 1 < B:
                        mx(b + 1, u)
                if b + 1 < B:
                    route(b + 1)
                if b + 2 < B:
                    proj(b + 2)
                tail(b)
                if b + 1 < B:
                    pre(b + 1)

        ROWS = 16 * 3 * len(COMBOS)
        block = ctx.enter_context(nc.Block())

        @block.sync
        def _(sp):
            def load(dst, src, s):
                sp.dma_start(dst, src).then_inc(s, 16)

            def load_xT(b):
                load(xT_s[:, b % 2], x_T[:, :, b * T:(b + 1) * T], ld_xT[b])

            def load_ctxT(b):
                load(ctxT_s[:, b % 2], ctx_T[:, b * T:(b + 1) * T], ld_ctxT[b])

            load(wqkv_s[:], w_qkv, ld["wqkv"])
            load_xT(0)
            load(xaw_s[:], xa_w, ld["xaw"])
            load_ctxT(0)
            load(xab_s[:], xa_b, ld["xab"])
            load(identb[:], c_identb, ld["identb"])
            load(mask[:], c_mask, ld["mask"])
            load_xT(1)
            load_ctxT(1)
            load(ident[:], c_ident, ld["ident"])
            load(wr_s[:], w_r, ld["wr"])
            load(w_in[:], w_ffn[0], ld_w)
            load(x_s[:], x_tok, ld["x"])
            load(wo_s[:], w_o, ld["wo"])
            load(lower[:], c_lower, ld["lower"])
            load(sel[:], c_sel, ld["sel"])


            def proj(b):
                i = b % 2
                if b < 2:
                    sp.wait_ge(init_qt, 1)
                    sp.wait_ge(init_p, (3, 6)[b])
                    sp.dma_start(KTp[i][MROW:MROW + 3, :, :], ones[:]).then_inc(ones_rows, 16)
                sp.wait_ge(parts_done, 2 * (b + 1))
                if b >= 2:
                    sp.wait_ge(st_done, SU * (b - 1))
                for c, (pq, pk) in enumerate(COMBOS):
                    r = slice(HD * c, HD * (c + 1))
                    sp.dma_start(QT[i][r, :, :], part_q[:, pq, :]).then_inc(qk_rows[i], 16)
                    sp.dma_start(KTs[i][r, :, :], part_k[:, pk, :]).then_inc(qk_rows[i], 16)
                    sp.dma_start(KTp[i][r, :, :], part_k[:, pk, :]).then_inc(qk_rows[i], 16)

            def route(b):
                sp.wait_ge(mrow_done, b + 1)
                sp.dma_start(QT[b % 2][MROW:MROW + 3, :, :], mrow[:]).then_inc(m_rows, 16)
                if b + 2 < B:
                    sp.wait_ge(proj_done, b + 1)
                    load_xT(b + 2)
                    sp.wait_ge(xqk_done, b + 1)
                    load_ctxT(b + 2)

            def nothing(*_):
                pass

            schedule(proj, nothing, nothing, route, nothing, nothing)
            for p in range(1, PAIRS):
                sp.wait_ge(whi_done, p)
                sp.wait_ge(wlo_done, p)
                load(w_in[:], w_ffn[p], ld_w)
            for b in range(B):
                sp.wait_ge(out_done, b + 1)
                sp.dma_start(out[b], x_s[:, b * TC:(b + 1) * TC, :]).then_inc(stored, 16)
            sp.wait_ge(stored, 16 * B)

        @block.tensor
        def _(pe):
            readers = {"M0": [], "M1": []}

            def take(name, *read_by):
                for s, value in readers[name]:
                    pe.wait_ge(s, value)
                readers[name] = list(read_by)

            def proj(b):
                if b == 0:
                    pe.wait_ge(ld["wqkv"], 16)
                pe.wait_ge(ld_xT[b], 16)
                take("M0", (parts_done, 2 * b + 1))
                take("M1", (v_done, 2 * (b + 1)), (parts_done, 2 * (b + 1)))
                xT = xT_s[:, b % 2]
                for h in range(2):
                    for c in range(DC):
                        pe.matmul(M0[:, h * T:(h + 1) * T], wqkv_s[:, c, h * P:(h + 1) * P], xT[:, c, :],
                                  start=(c == 0), stop=(c == DC - 1))
                for c in range(DC):
                    pe.matmul(M1[0:64, 0:T], wqkv_s[:, c, 256:320], xT[:, c, :],
                              start=(c == 0), stop=(c == DC - 1))
                for t in range(TC):
                    for c in range(DC):
                        last = pe.matmul(M1[:, T + 64 * t:T + 64 * (t + 1)],
                                         xT[:, c, P * t:P * (t + 1)], wqkv_s[:, c, 320:384],
                                         start=(c == 0), stop=(c == DC - 1))
                last.then_inc(proj_done, 1)

            def mx(b, u):
                i = b % 2
                n = SU * b + u
                if u == 0:
                    pe.wait_ge(qk_rows[i], ROWS * (b // 2 + 1))
                    if b == 0:
                        pe.wait_ge(ld["mask"], 16)
                        pe.wait_ge(ld["identb"], 16)
                if n >= 2:
                    pe.wait_ge(max_done, n - 1)
                o = SQ[n % 2]
                if u < 8:
                    pe.matmul(o[:, :], identb[:], mask[:, :, :], start=True, stop=False, skip_group_check=True)
                    for h in range(4):
                        last = pe.matmul(o[:, h * P:(h + 1) * P], QT[i][:, 4 * u + h, 0:P], KTs[i][:, u, 0:P],
                                         start=False, stop=True, skip_group_check=True)
                else:
                    h0 = 2 * (u - 8)
                    ov = o[:, :].rearrange("p (h k) -> p h k", h=2)
                    pe.matmul(ov[:, :, P:T], identb[:], mask[:, 0:2, :], start=True, stop=False,
                              skip_group_check=True)
                    for h in range(2):
                        last = pe.matmul(ov[:, h, :], QT[i][:, h0 + h, P:T], KTs[i][:, h0 // REP, :],
                                         start=False, stop=True, skip_group_check=True)
                last.then_inc(sq_done, 1)

            def route(b):
                pe.wait_ge(mparts_done, b + 1)
                take("M0", (mrow_done, b + 1))
                for q in range(TC):
                    last = pe.transpose(M0b[0:3 * NH, q * P:(q + 1) * P],
                                        part_m[:, q, :, :].rearrange("p a h -> p (a h)"), identb[:])
                last.then_inc(mT_done, 1)

            PARTS3 = ((0, 0), (0, 1), (1, 1))

            def times_v(b, quad, k3):
                kc, q = PARTS3[k3]
                n = 2 * b + quad
                if k3 == 0:
                    pe.wait_ge(exp_done, 12 * (n + 1))
                    pe.wait_ge(causal_done, 8 * (n + 1))
                    pe.wait_ge(v_done, 2 * (b + 1))
                    if n >= 1:
                        pe.wait_ge(oT_done, n)
                for j in range(4):
                    g = 4 * quad + j
                    last = pe.matmul(PV[q][32 * j:32 * (j + 1), :], V[b % 2][:, kc, g, :],
                                     probs[:, (8 * b + g) % RING, k3, :],
                                     start=(k3 < 2), stop=(k3 != 1), skip_group_check=True)
                if k3 == 2:
                    last.then_inc(pv_done, 1)

            def at(b, u):
                i = b % 2
                g, (kc, q) = u // 3, PARTS3[u % 3]
                n = SU * b + u
                if u == 0:
                    pe.wait_ge(m_rows, 16 * (b + 1))
                    if b == 0:
                        pe.wait_ge(ones_rows, 32)
                if n >= 2:
                    pe.wait_ge(exp_done, n - 1)
                pe.matmul(ST[n % 2][:, :], KTp[i][:, g, kc * P:(kc + 1) * P],
                          QT[i][:, REP * g:REP * (g + 1), q * P:(q + 1) * P], start=True, stop=True).then_inc(st_done, 1)
                if 14 <= u < 17:
                    times_v(b, 0, u - 14)

            def turn(b, quad):
                pe.wait_ge(oT_done, 2 * b + quad + 1)
                if b == 0 and quad == 0:
                    pe.wait_ge(ld["ident"], 16)
                for q in range(TC):
                    take(("M0", "M1")[q], (y_done, 4 * b + 2 * quad + q + 1))
                    for h in range(REP):
                        last = pe.transpose((M0, M1)[q][:, h * P:(h + 1) * P], oT[:, quad, q, h * P:(h + 1) * P], ident[:])
                    last.then_inc(ot_done, 1)

            def flip(src):
                for c in range(DC):
                    for q in range(TC):
                        last = pe.transpose(M0[:, c * T + q * P:c * T + (q + 1) * P], src[:, q, c * P:(c + 1) * P], ident[:])
                return last

            def times(lhsT, rhs):
                for q in range(TC):
                    for c in range(DC):
                        last = pe.matmul(M1[:, q * D:(q + 1) * D], lhsT[:, c, q * P:(q + 1) * P], rhs[:, c, :],
                                         start=(c == 0), stop=(c == DC - 1))
                return last

            def tail(b):
                for k3 in range(3):
                    times_v(b, 1, k3)
                turn(b, 0)
                turn(b, 1)
                pe.wait_ge(y_done, 4 * (b + 1))
                take("M0", (yT_done, b + 1))
                flip(y).then_inc(yt_done, 1)
                pe.wait_ge(yT_done, b + 1)
                if b == 0:
                    pe.wait_ge(ld["wo"], 16)
                take("M1", (res1_done, b + 1))
                times(yT, wo_s).then_inc(wo_done, 1)
                pe.wait_ge(x1_done, b + 1)
                take("M0", (x1T_done, b + 1))
                flip(x1).then_inc(x1t_done, 1)
                pe.wait_ge(x1T_done, b + 1)
                pe.wait_ge(attT_done, b + 1)
                take("M1", (res2_done, b + 1))
                times(x1T, attT).then_inc(xm_done, 1)
                pe.wait_ge(x2_done, b + 1)
                take("M0", (x2hi_done, b + 1), (x2lo_done, b + 1))
                flip(x2[:, b * TC:(b + 1) * TC, :]).then_inc(x2t_done, 1)
                pe.wait_ge(x2hi_done, b + 1)
                pe.wait_ge(x2lo_done, b + 1)
                if b == 0:
                    pe.wait_ge(wr_done, 2)
                take("M1", (lsub_done, b + 1))
                for q in range(TC):
                    tok = slice(b * T + q * P, b * T + (q + 1) * P)
                    n = 0
                    for xs, ws in ((x2T_hi, wr_hi), (x2T_hi, wr_lo), (x2T_lo, wr_hi)):
                        for c in range(DC):
                            last = pe.matmul(M1[:, q * E:(q + 1) * E], xs[:, c, tok], ws[:, c, :],
                                             start=(n == 0), stop=(n == 5))
                            n += 1
                last.then_inc(lg_done, 1)
                pe.wait_ge(gparts_done, b + 1)
                take("M0", (gateT_done, b + 1))
                for q in range(TC):
                    last = pe.transpose(M0b[0:3 * NW, q * P:(q + 1) * P],
                                        part_g[:, q, :, :].rearrange("p a e -> p (a e)"), identb[:])
                last.then_inc(gT_done, 1)

            def pre(b):
                pe.wait_ge(ld_ctxT[b], 16)
                if b == 0:
                    pe.wait_ge(ld["xaw"], 16)
                take("M0", (xqk_sb, 2 * (b + 1)))
                for j in range(2):
                    last = pe.matmul(M0[:, j * T:(j + 1) * T], xaw_s[:, j, :], ctxT_s[:, b % 2, :],
                                     start=True, stop=True)
                last.then_inc(xqk_done, 1)
                pe.wait_ge(xqk_sb, 2 * (b + 1))
                take("M1", (xexp_done, 2 * (b + 1)))
                for r in range(TC):
                    last = pe.matmul(M1[:, r * T:(r + 1) * T], xaqk[:, 0, r * P:(r + 1) * P], xaqk[:, 1, :],
                                     start=True, stop=True)
                last.then_inc(xen_done, 1)
                pe.wait_ge(xatt_done, 2 * (b + 1))
                if b == 0:
                    pe.wait_ge(ld["ident"], 16)
                take("M0", (attT_done, b + 1))
                flip(xae).then_inc(xat_done, 1)

            schedule(proj, pre, mx, route, at, tail)

            pe.wait_ge(oT_done, 2 * B)
            pe.wait_ge(max_done, SU * B)
            for k in range(4):
                pe.matmul(bank[k][:, :], zero[:, 0:P], zero[:, :], start=True, stop=False, skip_group_check=True)

            def gate_up(half, c, r, slot):
                f0, fn = CH[c]
                tok = slice(half * HALF, (half + 1) * HALF)
                for j, dst in ((0, G[r]), (1, U[r])):
                    n = 0
                    for ws, xs in ((w_hi, x2T_hi), (w_hi, x2T_lo), (w_lo, x2T_hi)):
                        for d in range(DC):
                            col = (j * DC + d) * FP + f0
                            last = pe.matmul(dst[0:fn, :], ws[slot][:, col:col + fn], xs[:, d, tok],
                                             start=(n == 0), stop=(n == 5))
                            n += 1
                last.then_inc(gu_done, 1)

            def spread(k, half, c, r):
                fn = CH[c][1]
                pe.matmul(G[r][0:fn, :], sel[:, k * P:k * P + fn],
                          gateT[:, half * HALF:(half + 1) * HALF], start=True, stop=True).then_inc(spread_done, 1)

            def down(half, c, r, slot):
                fn = CH[c][1]
                for t4 in range(HALF // P):
                    t = half * (HALF // P) + t4
                    for hs, ws in ((h_hi, w_hi), (h_hi, w_lo), (h_lo, w_hi)):
                        last = pe.matmul(bank[t // 2][:, (t % 2) * D:(t % 2 + 1) * D], hs[r][0:fn, t4 * P:(t4 + 1) * P],
                                         ws[slot][0:fn, GUW + c * D:GUW + (c + 1) * D],
                                         start=False, stop=False, skip_group_check=True)
                last.then_inc(down_done, 1)

            steps = [(p, h, c) for p in range(PAIRS) for h in range(NHALF) for c in range(NCH)]
            for s in range(STEPS + 2):
                if s < STEPS:
                    p, h, c = steps[s]
                    if (h, c) == (0, 0):
                        pe.wait_ge(whi_done, p + 1)
                        pe.wait_ge(wlo_done, p + 1)
                    if s == 0:
                        pe.wait_ge(gateT_done, B)
                    if s >= 2:
                        pe.wait_ge(hid_done, s - 1)
                    gate_up(h, c, s % 2, p % 2)
                if 1 <= s <= STEPS:
                    p, h, c = steps[s - 1]
                    if s == 1:
                        pe.wait_ge(ld["sel"], 16)
                    pe.wait_ge(silu_done, s)
                    spread(p * NCH + c, h, c, (s - 1) % 2)
                if s >= 2:
                    p, h, c = steps[s - 2]
                    pe.wait_ge(hhi_done, s - 1)
                    pe.wait_ge(hlo_done, s - 1)
                    down(h, c, s % 2, p % 2)

        @block.scalar
        def _(act):
            def copy(dst, src):
                return nc.scalar.activation(dst, src, ACT.Copy)

            def proj(b):
                act.wait_ge(proj_done, b + 1)
                if b >= 1:
                    act.wait_ge(qk_rows[(b - 1) % 2], ROWS * ((b - 1) // 2 + 1))
                copy(part_q[:, 0, :], M0[:, :]).then_inc(hi_done, 1)
                copy(part_k[:, 0, :], M1[0:64, 0:T]).then_inc(hi_done, 1)
                if b == 0:
                    act.wait_ge(init_v, 4)
                if b >= 2:
                    act.wait_ge(pv_done, 2 * (b - 1))
                for t in range(TC):
                    copy(V[b % 2][:, t, :, 0:HD],
                         M1[:, T + 64 * t:T + 64 * (t + 1)].rearrange("p (g d) -> p g d", g=NKV)).then_inc(v_done, 1)

            def mx(b, u):
                pass

            def route(b):
                act.wait_ge(mT_done, b + 1)
                if b >= 1:
                    act.wait_ge(m_rows, 16 * b)
                copy(mrow[:], M0b[0:3 * NH, 0:T]).then_inc(mrow_done, 1)

            def at(b, u):
                g, k = u // 3, u % 3
                n = SU * b + u
                slot = 8 * b + g
                if k == 0 and slot >= RING:
                    act.wait_ge(pv_done, (slot - RING) // 4 + 1)
                act.wait_ge(st_done, n + 1)
                nc.scalar.activation(probs[:, slot % RING, k, :], ST[n % 2][:, :], ACT.Exp,
                                     scale=SCALE).then_inc(exp_done, 1)
                if u == 18:
                    take_out(b, 0)

            def take_out(b, quad):
                act.wait_ge(pv_done, 2 * b + quad + 1)
                if b >= 1 and quad == 0:
                    act.wait_ge(ot_done, 4 * b)
                copy(oT[:, quad, 0, :], PV[0][:, :])
                copy(oT[:, quad, 1, :], PV[1][:, :]).then_inc(oT_done, 1)

            def tail(b):
                take_out(b, 1)
                act.wait_ge(yt_done, b + 1)
                if b >= 1:
                    act.wait_ge(wo_done, b)
                copy(yT[:, :, :].rearrange("p c t -> p (c t)"), M0[:, :]).then_inc(yT_done, 1)
                act.wait_ge(x1t_done, b + 1)
                if b >= 1:
                    act.wait_ge(xm_done, b)
                copy(x1T[:, :, :].rearrange("p c t -> p (c t)"), M0[:, :]).then_inc(x1T_done, 1)
                act.wait_ge(x2t_done, b + 1)
                copy(x2T_hi[:, :, b * T:(b + 1) * T], M0[:, :].rearrange("p (c t) -> p c t", c=DC)).then_inc(x2hi_done, 1)
                act.wait_ge(lsub_done, b + 1)
                nc.scalar.activation(lexp[:], lsub[:], ACT.Exp).then_inc(lexp_done, 1)
                act.wait_ge(gT_done, b + 1)
                copy(gateT[:, b * T:(b + 1) * T], M0b[0:3 * NW, 0:T]).then_inc(gateT_done, 1)

            def pre(b):
                act.wait_ge(xmax_done, b + 1)
                if b >= 1:
                    act.wait_ge(xat_done, b)
                for r in range(TC):
                    nc.scalar.activation(xae[:, r, :], M1[:, r * T:(r + 1) * T], ACT.Exp, bias=xam[:, r:r + 1],
                                         accum_out=xal[:, r:r + 1]).then_inc(xexp_done, 1)
                act.wait_ge(xat_done, b + 1)
                if b >= 1:
                    act.wait_ge(xm_done, b)
                copy(attT[:, :, :].rearrange("p c t -> p (c t)"), M0[:, :]).then_inc(attT_done, 1)

            schedule(proj, pre, mx, route, at, tail)

            def hidden_hi(s):
                r, fn = s % 2, CH[s % NCH][1]
                act.wait_ge(hid_done, s + 1)
                if s >= 2:
                    act.wait_ge(down_done, s - 1)
                copy(h_hi[r][0:fn, :], hid[r][0:fn, :]).then_inc(hhi_done, 1)

            for s in range(STEPS):
                r, fn = s % 2, CH[s % NCH][1]
                act.wait_ge(gu_done, s + 1)
                if s >= 2:
                    act.wait_ge(prod_done, s - 1)
                nc.scalar.activation(sg[r][0:fn, :], G[r][0:fn, :], ACT.Silu).then_inc(silu_done, 1)
                if s >= 1:
                    hidden_hi(s - 1)
            hidden_hi(STEPS - 1)

        @block.vector
        def _(v):
            ve = nc.vector
            own = [0]

            def step(ins):
                own[0] += 1
                return ins.then_inc(dve, 1)

            def settle():
                v.wait_ge(dve, own[0])

            ve.memset(QT[0][:, :, :].rearrange("p a b -> p (a b)").bitcast(F32), 0.0).then_inc(init_qt, 1)
            ve.memset(zero[:], 0.0).then_inc(init_v, 1)
            ve.memset(mhalf[:], -0.5).then_inc(init_v, 1)
            for i in range(2):
                step(ve.memset(V[i][:], 0.0))
            settle()
            for i in range(2):
                ve.memset(V[i][:, :, :, HD:HD + 1], 1.0).then_inc(init_v, 1)
            ve.memset(gatew[:, :, E:NW], 1.0).then_inc(init_v, 1)

            def proj(b):
                v.wait_ge(hi_done, 2 * (b + 1))
                if b >= 1:
                    v.wait_ge(parts_done, 2 * b)
                step(ve.tensor_tensor(rest_q[:], M0[:, :], part_q[:, 0, :], ALU.subtract))
                v.wait_ge(v_done, 2 * (b + 1))
                step(ve.tensor_tensor(rest_k[:], M1[0:64, 0:T], part_k[:, 0, :], ALU.subtract))
                settle()
                step(ve.tensor_copy(part_q[:, 1, :], rest_q[:]))
                step(ve.tensor_copy(part_k[:, 1, :], rest_k[:]))
                settle()
                ve.tensor_tensor(part_q[:, 2, :], rest_q[:], part_q[:, 1, :], ALU.subtract).then_inc(parts_done, 1)
                ve.tensor_tensor(part_k[:, 2, :], rest_k[:], part_k[:, 1, :], ALU.subtract).then_inc(parts_done, 1)

            def mx(b, u):
                n = SU * b + u
                v.wait_ge(sq_done, n + 1)
                if u < 8:
                    o, src = negmax[:, 0, 4 * u:4 * u + 4], SQ[n % 2][:, :].rearrange("p (h k) -> p h k", h=4)
                else:
                    h0 = 2 * (u - 8)
                    o, src = negmax[:, 1, h0:h0 + 2], SQ[n % 2][:, :].rearrange("p (h k) -> p h k", h=2)
                ve.tensor_reduce(o, src, AX_X, ALU.max, negate=True).then_inc(max_done, 1)

            def route(b):
                v.wait_ge(max_done, SU * (b + 1))
                if b >= 1:
                    v.wait_ge(mT_done, b)
                    v.wait_ge(mparts_done, b)
                step(ve.tensor_copy(part_m[:, :, 0, :], negmax[:]))
                settle()
                step(ve.tensor_tensor(rest_m[:], negmax[:], part_m[:, :, 0, :], ALU.subtract))
                settle()
                step(ve.tensor_copy(part_m[:, :, 1, :], rest_m[:]))
                settle()
                ve.tensor_tensor(part_m[:, :, 2, :], rest_m[:], part_m[:, :, 1, :], ALU.subtract).then_inc(mparts_done, 1)

            def at(b, u):
                pass

            def normalise(b, quad):
                for q in range(TC):
                    v.wait_ge(ot_done, 4 * b + 2 * quad + q + 1)
                    m = (M0, M1)[q][:, :].rearrange("p (h j c) -> p h j c", h=REP, j=4)
                    if b or quad or q:
                        v.wait_ge(y_done, 4 * b + 2 * quad + q)
                    step(ve.reciprocal(rden[:, :].rearrange("p (h j) -> p h j", h=REP), m[:, :, :, HD]))
                    settle()
                    if b >= 1:
                        v.wait_ge(yt_done, b)
                    o = y[:, q, quad * P:(quad + 1) * P].rearrange("p (j h d) -> p h j d", j=4, h=REP)
                    den = rden[:, :].rearrange("p (h j o) -> p h j o", h=REP, o=1).to_broadcast([P, REP, 4, HD])
                    ve.tensor_tensor(o, m[:, :, :, 0:HD], den, ALU.mult).then_inc(y_done, 1)

            norms = [0]

            def layernorm(dst, src, done, value):
                for q in range(TC):
                    step(ve.bn_stats(stat[:, q, :], src[:, q, :]))
                settle()
                for q in range(TC):
                    step(ve.bn_aggr(mv[:, q, :], stat[:, q, :]))
                settle()
                norms[0] += 1
                ve.tensor_scalar(veps[:], mv[:, :, 1], EPS, None, ALU.add).then_inc(var_done, 1)
                v.wait_ge(rstd_done, norms[0])
                for q in range(TC):
                    last = ve.tensor_scalar(dst[:, q, :], src[:, q, :], mv[:, q, 0:1], rstd[:, q:q + 1],
                                            ALU.subtract, ALU.mult)
                    if q < TC - 1:
                        step(last)
                last.then_inc(done, 1)
                v.wait_ge(done, value)

            def tail(b):
                normalise(b, 0)
                normalise(b, 1)
                if b == 0:
                    v.wait_ge(ld["x"], 16)
                v.wait_ge(wo_done, b + 1)
                ve.tensor_tensor(res[:, :, :].rearrange("p q d -> p (q d)"), M1[:, :],
                                 x_s[:, b * TC:(b + 1) * TC, :].rearrange("p q d -> p (q d)"), ALU.add).then_inc(res1_done, 1)
                v.wait_ge(res1_done, b + 1)
                if b >= 1:
                    v.wait_ge(x1t_done, b)
                layernorm(x1, res, x1_done, b + 1)
                v.wait_ge(xm_done, b + 1)
                ve.tensor_tensor(res[:, :, :].rearrange("p q d -> p (q d)"), M1[:, :],
                                 x1[:, :, :].rearrange("p q d -> p (q d)"), ALU.add).then_inc(res2_done, 1)
                v.wait_ge(res2_done, b + 1)
                layernorm(x2[:, b * TC:(b + 1) * TC, :], res, x2_done, b + 1)
                v.wait_ge(x2hi_done, b + 1)
                ve.tensor_tensor(x2T_lo[:, :, b * T:(b + 1) * T], M0[:, :].rearrange("p (c t) -> p c t", c=DC),
                                 x2T_hi[:, :, b * T:(b + 1) * T].bitcast(F32), ALU.subtract).then_inc(x2lo_done, 1)
                router(b)

            def router(b):
                v.wait_ge(lg_done, b + 1)
                logits = M1[:, 0:TC * E].rearrange("p (q e) -> p q e", q=TC)
                per = lambda a: a[:, :].rearrange("p (q o) -> p q o", o=1).to_broadcast([P, TC, E])
                step(ve.tensor_reduce(lmax[:], logits, AX_X, ALU.max))
                settle()
                ve.tensor_tensor(lsub[:], logits, per(lmax), ALU.subtract).then_inc(lsub_done, 1)
                v.wait_ge(lexp_done, b + 1)
                step(ve.tensor_reduce(lsum[:], lexp[:], AX_X, ALU.add))
                settle()
                step(ve.reciprocal(lsum[:], lsum[:]))
                settle()
                step(ve.tensor_tensor(score[:], lexp[:], per(lsum), ALU.mult))
                settle()
                if b == 0:
                    v.wait_ge(ld["lower"], 16)
                for q in range(TC):
                    mine = score[:, q, :].rearrange("p (e o) -> p e o", o=1).to_broadcast([P, E, E])
                    other = score[:, q, :].rearrange("p (o j) -> p o j", o=1).to_broadcast([P, E, E])
                    step(ve.tensor_tensor(above[:, q], other, mine, ALU.is_gt))
                    step(ve.tensor_tensor(equal[:, q], other, mine, ALU.is_equal))
                settle()
                for q in range(TC):
                    step(ve.tensor_tensor(equal[:, q], equal[:, q], lower[:], ALU.mult))
                settle()
                step(ve.tensor_tensor(above[:], above[:], equal[:], ALU.add))
                settle()
                step(ve.tensor_reduce(rank[:], above[:], AX_X, ALU.add))
                settle()
                step(ve.scalar_tensor_tensor(gatew[:, :, 0:E], rank[:], 2.0, score[:], ALU.is_lt, ALU.mult))
                settle()
                if b >= 1:
                    v.wait_ge(gT_done, b)
                    v.wait_ge(gparts_done, b)
                if b == 0:
                    v.wait_ge(init_v, 5)
                step(ve.tensor_copy(part_g[:, :, 0, :], gatew[:]))
                settle()
                step(ve.tensor_tensor(rest_g[:], gatew[:], part_g[:, :, 0, :], ALU.subtract))
                settle()
                step(ve.tensor_copy(part_g[:, :, 1, :], rest_g[:]))
                settle()
                ve.tensor_tensor(part_g[:, :, 2, :], rest_g[:], part_g[:, :, 1, :], ALU.subtract).then_inc(gparts_done, 1)

            def weights_hi(p):
                v.wait_ge(ld_w, 16 * (p + 1))
                ve.tensor_copy(w_hi[p % 2][:], w_in[:]).then_inc(whi_done, 1)

            def pre(b):
                if b == 1:
                    weights_hi(0)
                if b == 0:
                    v.wait_ge(ld["wr"], 16)
                    ve.tensor_copy(wr_hi[:], wr_s[:]).then_inc(wr_done, 1)
                    v.wait_ge(wr_done, 1)
                    ve.tensor_tensor(wr_lo[:], wr_s[:], wr_hi[:].bitcast(F32), ALU.subtract).then_inc(wr_done, 1)
                    v.wait_ge(ld["xab"], 16)
                v.wait_ge(xqk_done, b + 1)
                if b >= 1:
                    v.wait_ge(xen_done, b)
                    v.wait_ge(xatt_done, 2 * b)
                for j in range(2):
                    ve.tensor_scalar(xaqk[:, j, :], M0[:, j * T:(j + 1) * T], xab_s[:, j:j + 1], None,
                                     ALU.add).then_inc(xqk_sb, 1)
                v.wait_ge(xen_done, b + 1)
                if b >= 1:
                    v.wait_ge(xexp_done, 2 * b)
                ve.tensor_reduce(xam[:], M1[:, :].rearrange("p (r k) -> p r k", r=TC), AX_X, ALU.max,
                                 negate=True).then_inc(xmax_done, 1)
                v.wait_ge(xexp_done, 2 * (b + 1))
                step(ve.reciprocal(xar[:], xal[:]))
                settle()
                for r in range(TC):
                    ve.tensor_scalar(xae[:, r, :], xae[:, r, :], xar[:, r:r + 1], None, ALU.mult).then_inc(xatt_done, 1)

            schedule(proj, pre, mx, route, at, tail)

            for s in range(STEPS):
                r, fn = s % 2, CH[s % NCH][1]
                if s == 1:
                    weights_hi(1)
                if s % PSTEPS == 2 and 2 <= s // PSTEPS + 1 < PAIRS:
                    v.wait_ge(down_done, s - 2)
                    weights_hi(s // PSTEPS + 1)
                v.wait_ge(silu_done, s + 1)
                if s >= 2:
                    v.wait_ge(hid_done, s - 1)
                ve.tensor_tensor(gu[r][0:fn, :], U[r][0:fn, :], sg[r][0:fn, :], ALU.mult).then_inc(prod_done, 1)
                v.wait_ge(prod_done, s + 1)
                v.wait_ge(spread_done, s + 1)
                if s >= 2:
                    v.wait_ge(hhi_done, s - 1)
                    v.wait_ge(hlo_done, s - 1)
                ve.tensor_tensor(hid[r][0:fn, :], G[r][0:fn, :], gu[r][0:fn, :], ALU.mult).then_inc(hid_done, 1)

            v.wait_ge(down_done, STEPS)
            for b in range(B):
                step(ve.tensor_tensor(res[:, :, :].rearrange("p q d -> p (q d)"), bank[b][:, :],
                                      x2[:, b * TC:(b + 1) * TC, :].rearrange("p q d -> p (q d)"), ALU.add))
                settle()
                layernorm(x_s[:, b * TC:(b + 1) * TC, :], res, out_done, b + 1)

        @block.gpsimd
        def _(pool):
            gp = nc.gpsimd
            gp.memset(ones[:], 1.0).then_inc(init_p, 1)
            for tile in (KTs[0], KTp[0], KTs[1], KTp[1], QT[1]):
                gp.memset(tile[:, :, :].rearrange("p a b -> p (a b)").bitcast(F32), 0.0).then_inc(init_p, 1)
            norms = [0]

            def rsqrt():
                if norms[0] == 0:
                    pool.wait_ge(init_v, 2)
                norms[0] += 1
                pool.wait_ge(var_done, norms[0])
                gp.tensor_tensor(rstd[:], veps[:], mhalf[:], ALU.pow).then_inc(rstd_done, 1)

            def at(b, u):
                if u % 3 == 1:
                    return
                pool.wait_ge(exp_done, SU * b + u + 1)
                t = probs[:, (8 * b + u // 3) % RING, u % 3, :].rearrange("p (h q) -> p h q", h=REP)
                gp.affine_select(out=t, in_=t, compare_op=ALU.is_ge, fill=0.0, base=0,
                                 pattern=[[0, REP], [1, P]], channel_multiplier=-1).then_inc(causal_done, 1)

            def tail(b):
                rsqrt()
                rsqrt()

            def weights_lo(p):
                pool.wait_ge(whi_done, p + 1)
                gp.tensor_tensor(w_lo[p % 2][:], w_in[:], w_hi[p % 2][:].bitcast(F32), ALU.subtract).then_inc(wlo_done, 1)

            def pre(b):
                if b == 1:
                    weights_lo(0)

            def nothing(*_):
                pass

            schedule(nothing, pre, nothing, nothing, at, tail)

            for s in range(STEPS):
                r, fn = s % 2, CH[s % NCH][1]
                if s == 1:
                    weights_lo(1)
                if s % PSTEPS == 2 and 2 <= s // PSTEPS + 1 < PAIRS:
                    weights_lo(s // PSTEPS + 1)
                pool.wait_ge(hhi_done, s + 1)
                if s >= 2:
                    pool.wait_ge(down_done, s - 1)
                gp.tensor_tensor(h_lo[r][0:fn, :], hid[r][0:fn, :], h_hi[r][0:fn, :].bitcast(F32),
                                 ALU.subtract).then_inc(hlo_done, 1)
            for _ in range(B):
                rsqrt()


def constants():
    bf = np.dtype("bfloat16")
    ident = np.eye(P, dtype=np.float32)
    later = np.arange(P)[None, :] > np.arange(P)[:, None]
    mask = np.repeat(np.where(later, MASKED, 0.0)[:, None, :], REP, axis=1).astype(bf)
    sel = np.zeros((3, NW, PAIRS, NCH, P), np.float32)
    for p in range(PAIRS):
        for c, (f0, fn) in enumerate(CH):
            for f in range(fn):
                sel[:, E if p == PAIRS - 1 else 2 * p + (f0 + f) // FE, p, c, f] = 1.0
    lower = np.tile(np.tril(np.ones((E, E), np.float32), -1), (P, 1, 1))
    return {"c_ident": ident, "c_identb": ident.astype(bf), "c_mask": mask,
            "c_sel": sel.reshape(3 * NW, PAIRS * NCH * P).astype(bf), "c_lower": lower}


def rows(a, chunks):
    return np.ascontiguousarray(a.reshape(chunks, P, -1).transpose(1, 0, 2))


def kernel(**inputs):
    from concourse import bacc
    from concourse.bass_utils import run_bass_kernel_spmd

    a = {k: np.asarray(v) for k, v in inputs.items()}
    x = a["x"].reshape(B * T, D)
    wq = a["L0_attn_wq"].reshape(D, NH // 2, 2, HD).transpose(0, 2, 3, 1).reshape(D, NH * HD)
    wk = a["L0_attn_wk"].reshape(D, NKV, HD).transpose(0, 2, 1).reshape(D, NKV * HD)
    w_ffn = np.zeros((PAIRS, P, WW), np.float32)
    for p in range(PAIRS):
        if p < PAIRS - 1:
            g, u = (a[n][2 * p:2 * p + 2].reshape(FP, D) for n in ("L0_ffn_Wg", "L0_ffn_Wu"))
            d = a["L0_ffn_Wd"][2 * p:2 * p + 2].transpose(0, 2, 1).reshape(FP, D)
        else:
            g, u, d = a["L0_ffn_Wsg"], a["L0_ffn_Wsu"], a["L0_ffn_Wsd"].T
        for j, w in enumerate((g, u)):
            w_ffn[p, :, j * DC * FP:(j + 1) * DC * FP] = rows(np.ascontiguousarray(w.T), DC).reshape(P, DC * FP)
        for c, (f0, fn) in enumerate(CH):
            w_ffn[p, :fn, GUW + c * D:GUW + (c + 1) * D] = d[f0:f0 + fn]
    arrays = {
        "x_tok": rows(x, B * TC),
        "x_T": rows(np.ascontiguousarray(x.T), DC),
        "ctx_T": np.ascontiguousarray(a["ctx_1024"].reshape(B * T, CTX).T),
        "w_qkv": rows(np.concatenate([wq, wk, a["L0_attn_wv"]], axis=1), DC),
        "w_o": rows(a["L0_attn_wo"], DC),
        "xa_w": np.ascontiguousarray(np.stack([a["L0_xattn_Wq"].T, a["L0_xattn_Wk"].T], axis=1)),
        "xa_b": np.ascontiguousarray(np.stack([a["L0_xattn_bq"], a["L0_xattn_bk"]], axis=1)),
        "w_r": rows(np.ascontiguousarray(a["L0_ffn_Wr"].T), DC),
        "w_ffn": w_ffn,
        **constants(),
    }
    nc = bacc.Bacc("TRN2", target_bir_lowering=False, num_devices=1)
    args = [nc.dram_tensor(n, v.shape, mybir.dt.from_np(v.dtype), kind="ExternalInput").ap() for n, v in arrays.items()]
    out = nc.dram_tensor("out", (B, P, TC, D), F32, kind="ExternalOutput").ap()
    build_layer(nc, *args, out)
    r = run_bass_kernel_spmd(nc, [arrays], core_ids=[0])
    return np.asarray(r.results[0]["out"]).transpose(0, 2, 1, 3).reshape(B, T, D)
```

```python
from contextlib import ExitStack

import numpy as np

import concourse.bass as bass
from concourse import mybir

F32 = mybir.dt.float32
F32R = mybir.dt.float32r
BF16 = mybir.dt.bfloat16
ACT = mybir.ActivationFunctionType
ALU = mybir.AluOpType
AX_X = mybir.AxisListType.X

P = 128
B, T, D = 4, 256, 256
TC = T // P
DC = D // P
NH, NKV, HD = 32, 8, 8
REP = NH // NKV
CTX = 128
E, FE, FS = 8, 176, 352
F = E * FE + FS
NCH = -(-F // P)
FN = [min(P, F - c * P) for c in range(NCH)]
HALF = 512
NHALF = B * T // HALF
WRING = 6
WOWN = 3
EPS = 1e-5
MASKED = -3e38
SCALE = float(HD) ** -0.5
COMBOS = [(0, 0), (0, 1), (1, 0), (1, 1), (0, 2), (2, 0)]
MROW = len(COMBOS) * HD
GUW = 2 * DC * P
WW = GUW + D
NW = E + 1
RING = 6
WARM_LOAD, WARM_ROWS = 8, 14
SU = 24


EARLY = WRING
LATE = 2
STEP = [(c, h) for h in range(NHALF) for c in range(EARLY)]
STEP += [(c, h) for c in range(EARLY, NCH - LATE) for h in range(NHALF)]
STEP += [(c, h) for h in range(NHALF) for c in range(NCH - LATE, NCH)]
STEPS = len(STEP)


MX = [(-7.812, 0.8019), (7.319, 0.4056), (6.316, 0.4965)]
START = [
    (0.762, "proj", 0, 0), (1.201, "PROJ", 0, 0), (2.84, "turn_v", 0, 0), (7.637, "TURN_V", 0, 0),
    (48.044, "PROJ", 1, 0), (48.258, "proj", 1, 0), (73.363, "MAX_PARTS", 0, 0), (95.228, "route", 0, 0),
    (98.127, "ROUTE", 0, 0),
]
BODY_0 = [
    (9.548, "xa_qk", 0, 0), (10.242, "XA_QK", 0, 0), (13.854, "times_v", 0, 0), (13.928, "xa_energy", 0, 0),
    (15.923, "MAX_PARTS", 1, 0), (16.822, "XA_ENERGY", 0, 0), (16.907, "ROUTE", 1, 0), (17.649, "times_v", 0, 1),
    (17.882, "route", 1, 0), (18.153, "TIMES_V", 0, 0), (18.263, "times_v", 0, 2), (19.675, "XA_SCALE", 0, 0),
    (20.098, "xa_flip", 0, 0), (20.947, "turn_v", 1, 0), (20.97, "TURN_V", 1, 0), (21.173, "XA_FLIP", 0, 0),
    (22.342, "PROJ", 2, 0), (23.049, "WEIGHTS", 0, 0), (27.114, "proj", 2, 0),
]
BODY_1 = [
    (-4.943, "times_v", -1, 3), (1.219, "times_v", -1, 4), (1.528, "turn", -1, 0), (2.061, "times_v", -1, 5),
    (3.102, "turn_gate", -2, 0), (3.5, "TIMES_V", -1, 1), (3.583, "TURN_GATE", -2, 0), (4.465, "TURN", -1, 0),
    (5.404, "turn", -1, 1), (6.542, "TURN", -1, 1), (9.276, "flip_y", -1, 0), (9.875, "FLIP_Y", -1, 0),
    (10.245, "wo", -1, 0), (11.312, "NORM1", -1, 0), (11.457, "xa_qk", 0, 0), (11.971, "XA_QK", 0, 0),
    (12.178, "times_v", 0, 0), (12.287, "xa_energy", 0, 0), (12.447, "NORM1", -1, 1), (13.394, "times_v", 0, 1),
    (16.046, "XA_ENERGY", 0, 0), (16.31, "FLIP_X1", -1, 0), (16.315, "times_v", 0, 2), (16.323, "flip_x1", -1, 0),
    (18.258, "TIMES_V", 0, 0), (18.924, "xm", -1, 0), (19.478, "XA_SCALE", 0, 0), (19.522, "NORM2", -1, 0),
    (19.807, "XA_FLIP", 0, 0), (20.132, "xa_flip", 0, 0), (20.785, "MAX_PARTS", 1, 0), (20.787, "NORM2", -1, 1),
    (22.289, "turn_v", 1, 0), (22.311, "TURN_V", 1, 0), (22.478, "ROUTE", 1, 0), (23.219, "route", 1, 0),
    (23.229, "WEIGHTS", 0, 0), (23.46, "PROJ", 2, 0), (24.081, "proj", 2, 0), (25.566, "flip_x2", -1, 0),
    (25.629, "FLIP_X2", -1, 0), (26.368, "LOGITS", -1, 0), (27.122, "SCORES", -1, 0), (29.771, "GATES", -1, 0),
    (31.63, "logits", -1, 0),
]
BODY_3 = [
    (-1.021, "times_v", -1, 3), (0.61, "times_v", -1, 4), (1.149, "TURN", -1, 0), (1.406, "TURN_GATE", -2, 0),
    (2.287, "turn_gate", -2, 0), (2.385, "times_v", -1, 5), (3.279, "turn", -1, 0), (3.5, "TIMES_V", -1, 1),
    (4.584, "turn", -1, 1), (6.203, "flip_y", -1, 0), (7.341, "FLIP_Y", -1, 0), (9.54, "wo", -1, 0),
    (10.005, "TURN", -1, 1), (11.226, "NORM1", -1, 0), (11.511, "xa_qk", 0, 0), (12.208, "XA_QK", 0, 0),
    (12.881, "times_v", 0, 0), (13.03, "xa_energy", 0, 0), (14.183, "times_v", 0, 1), (17.282, "XA_ENERGY", 0, 0),
    (17.758, "times_v", 0, 2), (18.121, "XA_SCALE", 0, 0), (19.165, "NORM1", -1, 1), (19.6, "TIMES_V", 0, 0),
    (20.61, "xa_flip", 0, 0), (22.191, "XA_FLIP", 0, 0),
]
BODY = [BODY_0, BODY_1, BODY_1, BODY_3]
FIRST_STEPS = [
    (-10.161, "flip_x1", 2, 0), (-4.316, "FLIP_X1", 2, 0), (-4.095, "WEIGHTS", 3, 0), (-2.412, "TURN", 3, 0),
    (-1.124, "times_v", 3, 3), (-1.124, "times_v", 3, 4), (-1.124, "times_v", 3, 5), (-0.813, "turn", 3, 0),
    (-0.265, "TIMES_V", 3, 1), (-0.226, "turn", 3, 1), (0.507, "xm", 2, 0), (0.618, "TURN", 3, 1),
    (0.871, "flip_y", 3, 0), (1.212, "wo", 3, 0), (1.217, "NORM2", 2, 0), (1.475, "NORM2", 2, 1),
    (1.655, "WEIGHTS", 4, 0), (1.686, "flip_x2", 2, 0), (1.887, "FLIP_Y", 3, 0), (2.106, "NORM1", 3, 0),
    (3.18, "open", 0, 0), (4.713, "FLIP_X2", 2, 0), (5.128, "NORM1", 3, 1), (5.207, "logits", 2, 0),
    (6.38, "WEIGHTS", 5, 0), (6.983, "LOGITS", 2, 0), (8.274, "flip_x1", 3, 0), (8.366, "FLIP_X1", 3, 0),
    (8.967, "SCORES", 2, 0), (9.598, "GATES", 2, 0), (9.724, "xm", 3, 0), (9.841, "turn_gate", 2, 0),
    (11.056, "NORM2", 3, 0), (12.299, "flip_x2", 3, 0), (12.592, "TURN_GATE", 2, 0), (13.425, "NORM2", 3, 1),
    (16.042, "logits", 3, 0), (16.391, "FLIP_X2", 3, 0), (17.173, "LOGITS", 3, 0), (18.806, "TURN_GATE", 3, 0),
    (18.903, "SCORES", 3, 0), (19.038, "GATES", 3, 0), (20.439, "turn_gate", 3, 0), (25.9, "open", 1, 0),
]
FFN = [
    (0.093, "gate_up", 0, 0), (0.995, "gate_up", 0, 1), (1.6, "SILU", 0, 0), (4.088, "PROD", 0, 0),
    (5.152, "spread", 0, 0), (5.3, "HID", 0, 0), (5.4, "HID_HI", 0, 0), (5.5, "HID_LO", 0, 0), (9.009, "down", 0, 0),
]
LAST = [[(1.741, "STORE", 0, 0), (12.538, "LAST_NORM", 0, 0), (13.398, "LAST_NORM", 0, 1)],
        [(8.6, "LAST_NORM", 0, 0), (9, "LAST_NORM", 0, 1), (9.1, "STORE", 0, 0)]]


def program_order():
    placed = []

    def put(base, entries, b=0):
        placed.extend((base + pos, len(placed) + k, name, b + db, u) for k, (pos, name, db, u) in enumerate(entries))

    put(-100, START)
    put(-100, [(50 + u, "mx", 0, u) for u in range(SU)])
    for b in range(B):
        put(100 * b, [(u, "at", b, u) for u in range(SU)])
        if b + 1 < B:
            m0, rate = MX[b]
            put(100 * b, [(m0 + rate * u, "mx", b + 1, u) for u in range(SU)])
        put(100 * b, [e for e in BODY[b] if 0 <= b + e[2] < B], b)
    put(100 * B, FIRST_STEPS)
    for n in range(STEPS):
        put(100 * B + 3 * n, FFN, n)
    for c in range(WRING, NCH):
        put(100 * B + 3 * STEP.index((c - WRING, NHALF - 1)) + 9.5, [(0, "WEIGHTS", c, 0)])
    for h in range(NHALF):
        put(100 * B + 3 * STEP.index((NCH - 1, h)), LAST[h], h)
    return [x[2:] for x in sorted(placed)]


def build_layer(nc, x_tok, x_T, ctx_T, w_qkv, w_o, xa_w, xa_b, w_r, w_ffn,
                c_ident, c_identb, c_mask, c_sel, c_lower, out):
    with ExitStack() as ctx:
        def sb(name, shape, dt=F32):
            return ctx.enter_context(nc.sbuf_tensor(name, shape, dt))

        def sem(name):
            return ctx.enter_context(nc.semaphore(name))

        ident = sb("ident", [P, P])
        identb = sb("identb", [P, P], BF16)
        mask = sb("mask", [P, REP, P], BF16)
        sel = sb("sel", [3 * NW, NCH * P], BF16)
        lower = sb("lower", [P, E, E])
        wqkv_s = sb("wqkv_s", [P, DC, NH * HD + 2 * NKV * HD])
        wo_s = sb("wo_s", [P, DC, D])
        xaw_s = sb("xaw_s", [P, 2, P])
        xab_s = sb("xab_s", [P, 2])
        wr_s = sb("wr_s", [P, DC, E])
        wr_hi = sb("wr_hi", [P, DC, E], F32R)
        wr_lo = sb("wr_lo", [P, DC, E], F32R)
        x_s = sb("x_s", [P, B * TC, D])
        xT_s = sb("xT_s", [P, 2, DC, T])
        ctxT_s = sb("ctxT_s", [P, 2, T])
        rest_k = sb("rest_k", [P, T])
        vT = sb("vT", [NKV * HD, T])
        part_q = sb("part_q", [P, 3, 2 * T], BF16)
        part_k = sb("part_k", [P, 3, T], BF16)
        KT = [sb(f"KT{i}", [P, NKV, T], BF16) for i in range(2)]
        V = [sb(f"V{i}", [P, TC, NKV, 32]) for i in range(2)]
        negmax = sb("negmax", [P, TC, NH])
        rest_m = sb("rest_m", [P, TC, NH])
        ones = sb("ones", [3, NKV * T], BF16)
        part_m = sb("part_m", [P, TC, 3, NH], BF16)
        mrow = sb("mrow", [3 * NH, T], BF16)
        oT = sb("oT", [P, 2, TC, 512])
        rden = sb("rden", [P, REP * 4])
        y = sb("y", [P, TC, D])
        yT = sb("yT", [P, DC, T])
        res = sb("res", [P, TC, D])
        rest_q = res[:, :, :].rearrange("p q d -> p (q d)")
        x1 = sb("x1", [P, TC, D])
        x1T = sb("x1T", [P, DC, T])
        stat = sb("stat", [P, 2 * TC, 6])
        mv = sb("mv", [P, 2 * TC, 2])
        veps = sb("veps", [P, 2 * TC])
        rstd = sb("rstd", [P, 2 * TC])
        mhalf = sb("mhalf", [P, 2 * TC])
        xaqk = sb("xaqk", [P, 2, T])
        xam = sb("xam", [P, TC])
        xae = sb("xae", [P, TC, T])
        xal = sb("xal", [P, TC])
        xar = sb("xar", [P, TC])
        attT = [sb(f"attT{i}", [P, TC, T]) for i in range(2)]
        x2 = sb("x2", [P, B * TC, D])
        x2T_hi = sb("x2T_hi", [P, DC, B * T], F32R)
        x2T_lo = sb("x2T_lo", [P, DC, B * T], F32R)
        lmax = sb("lmax", [P, TC])
        lexp = sb("lexp", [P, TC, E])
        lsum = sb("lsum", [P, TC])
        score = sb("score", [P, TC, E])
        above = sb("above", [P, TC, E, E])
        equal = sb("equal", [P, TC, E, E])
        lsub = sb("lsub", [P, TC, E])
        rank = sb("rank", [P, TC, E])
        gatew = sb("gatew", [P, TC, NW])
        rest_g = sb("rest_g", [P, TC, NW])
        part_g = sb("part_g", [P, TC, 3, NW], BF16)
        gateT = sb("gateT", [3 * NW, B * T], BF16)
        w_in = sb("w_in", [P, 2, WW])
        w_hi = [sb(f"w_hi{i}", [P, WW], F32R) for i in range(WOWN)]
        w_lo = [sb(f"w_lo{i}", [P, WW], F32R) for i in range(WOWN)]
        zero = sb("zero", [P, 512], BF16)
        with ExitStack() as attention:
            probs = attention.enter_context(nc.sbuf_tensor("probs", [P, RING, 3, 512], F32))
            QT = [attention.enter_context(nc.sbuf_tensor(f"QT{i}", [P, NH, T], BF16)) for i in range(2)]
        sg = [sb(f"sg{i}", [P, HALF]) for i in range(2)]
        gu = [sb(f"gu{i}", [P, HALF]) for i in range(2)]
        hid = [sb(f"hid{i}", [P, HALF]) for i in range(2)]
        h_hi = [sb(f"h_hi{i}", [P, HALF], F32R) for i in range(2)]
        h_lo = [sb(f"h_lo{i}", [P, HALF], F32R) for i in range(2)]
        res_l = sb("res_l", [P, 2 * TC, D])
        w_hi += [sb(f"w_hi{i}", [P, WW], F32R) for i in range(WOWN, WRING)]
        w_lo += [sb(f"w_lo{i}", [P, WW], F32R) for i in range(WOWN, WRING)]

        bank = [ctx.enter_context(nc.psum_tensor(f"bank{i}", [P, 512], F32)) for i in range(8)]
        ST = bank[0:2]
        SQ = bank[2:4]
        PV = bank[4:6]
        M0, M1 = bank[6:8]
        GU = [(bank[4], bank[5]) if n % 2 == 0 else (bank[2], bank[3]) if n < EARLY else (M0, M1) for n in range(STEPS)]
        M0b = M0[:, :].bitcast(BF16)

        ld = {n: sem(f"ld_{n}") for n in ("ident", "identb", "mask", "sel", "lower", "wqkv", "wo", "xaw", "xab",
                                          "wr", "x")}
        ld_xT = [sem(f"ld_xT{b}") for b in range(B)]
        ld_ctxT = [sem(f"ld_ctxT{b}") for b in range(B)]
        ones_rows = sem("ones_rows")
        ld_w = [sem(f"ld_w{i}") for i in range(2)]
        init_v = sem("init_v")
        init_p = sem("init_p")
        init_qt = sem("init_qt")
        wr_done = sem("wr_done")
        proj_done = sem("proj_done")
        hi_done = sem("hi_done")
        vT_done = sem("vT_done")
        vt_done = sem("vt_done")
        v_done = sem("v_done")
        mid_done = sem("mid_done")
        parts_done = sem("parts_done")
        qk_rows = [sem(f"qk_rows{i}") for i in range(2)]
        sq_done = sem("sq_done")
        max_done = sem("max_done")
        mparts_done = sem("mparts_done")
        mT_done = sem("mT_done")
        mrow_done = sem("mrow_done")
        m_zero = sem("m_zero")
        m_rows = sem("m_rows")
        st_done = sem("st_done")
        exp_done = sem("exp_done")
        causal_done = sem("causal_done")
        pv_done = sem("pv_done")
        oT_done = sem("oT_done")
        ot_done = sem("ot_done")
        y_done = sem("y_done")
        yt_done = sem("yt_done")
        yT_done = sem("yT_done")
        wo_done = sem("wo_done")
        res1_done = sem("res1_done")
        res2_done = sem("res2_done")
        x1_done = sem("x1_done")
        x1t_done = sem("x1t_done")
        x1T_done = sem("x1T_done")
        xm_done = sem("xm_done")
        x2_done = sem("x2_done")
        x2t_done = sem("x2t_done")
        x2hi_done = sem("x2hi_done")
        x2lo_done = sem("x2lo_done")
        var_done = sem("var_done")
        rstd_done = sem("rstd_done")
        xqk_done = sem("xqk_done")
        xqk_sb = sem("xqk_sb")
        xen_done = sem("xen_done")
        xmax_done = sem("xmax_done")
        xexp_done = sem("xexp_done")
        xatt_done = sem("xatt_done")
        xat_done = sem("xat_done")
        attT_done = sem("attT_done")
        lg_done = sem("lg_done")
        lsub_done = sem("lsub_done")
        lexp_done = sem("lexp_done")
        gparts_done = sem("gparts_done")
        gT_done = sem("gT_done")
        gateT_done = sem("gateT_done")
        dve = sem("dve")
        whi_done = sem("whi_done")
        wlo_done = sem("wlo_done")
        gu_done = sem("gu_done")
        silu_done = sem("silu_done")
        spread_done = sem("spread_done")
        prod_done = sem("prod_done")
        hid_done = sem("hid_done")
        hhi_done = sem("hhi_done")
        hlo_done = sem("hlo_done")
        down_done = sem("down_done")
        sums_done = sem("sums_done")
        out_done = sem("out_done")
        stored = sem("stored")

        order = program_order()

        def write(stages):
            for name, b, u in order:
                if name in stages:
                    stages[name](b, u)

        ROWS = 16 * 2 * len(COMBOS)
        block = ctx.enter_context(nc.Block())

        @block.sync
        def _(sp):
            def load(dst, src, s):
                sp.dma_start(dst, src).then_inc(s, 16)

            def load_xT(b):
                load(xT_s[:, b % 2], x_T[:, :, b * T:(b + 1) * T], ld_xT[b])

            def load_ctxT(b):
                load(ctxT_s[:, b % 2], ctx_T[:, b * T:(b + 1) * T], ld_ctxT[b])

            load(wqkv_s[:], w_qkv, ld["wqkv"])
            load_xT(0)
            load(identb[:], c_identb, ld["identb"])
            load(mask[:], c_mask, ld["mask"])
            load(ident[:], c_ident, ld["ident"])
            load_xT(1)
            load(xaw_s[:], xa_w, ld["xaw"])
            load_ctxT(0)
            load(xab_s[:], xa_b, ld["xab"])
            load_ctxT(1)
            load(wr_s[:], w_r, ld["wr"])

            def rows(b):
                i = b % 2
                if b < 2:
                    sp.wait_ge(init_qt, 1)
                    sp.wait_ge(init_p, b + 2 + (b > 0))
                    sp.dma_start(KT[i][MROW:MROW + 3, :, :], ones[:]).then_inc(ones_rows, 16)
                else:
                    sp.wait_ge(st_done, SU * (b - 1))
                    sp.dma_start(QT[i][MROW:MROW + 3, :, :].rearrange("p a b -> p (a b)").rearrange("p (r n) -> p r n", n=512),
                                 zero[0:3, :].rearrange("p (o n) -> p o n", o=1).to_broadcast([3, NH * T // 512, 512])
                                 ).then_inc(m_zero, 16)
                for part, ready in enumerate((hi_done, mid_done, parts_done)):
                    sp.wait_ge(ready, 2 * (b + 1))
                    for c, (pq, pk) in enumerate(COMBOS):
                        r = slice(HD * c, HD * (c + 1))
                        if pk == part:
                            sp.dma_start(KT[i][r, :, :], part_k[64:, pk, :]).then_inc(qk_rows[i], 16)
                        if pq == part:
                            sp.dma_start(QT[i][r, :, :], part_q[:, pq, :]).then_inc(qk_rows[i], 16)
                if b == 0:
                    for c in range(2):
                        load(w_in[:, c], w_ffn[c], ld_w[c])
                    load(x_s[:], x_tok, ld["x"])
                    load(wo_s[:], w_o, ld["wo"])
                    load(lower[:], c_lower, ld["lower"])
                    load(sel[:], c_sel, ld["sel"])

            def max_rows(b):
                sp.wait_ge(mrow_done, b + 1)
                sp.dma_start(QT[b % 2][MROW:MROW + 3, :, :], mrow[:]).then_inc(m_rows, 16)
                if b + 2 < B:
                    load_xT(b + 2)
                if 1 <= b < B - 1:
                    sp.wait_ge(xqk_done, b)
                    load_ctxT(b + 1)

            def weights(c):
                if c + 2 < NCH:
                    sp.wait_ge(whi_done, c + 1)
                    sp.wait_ge(wlo_done, c + 1)
                    load(w_in[:, c % 2], w_ffn[c + 2], ld_w[c % 2])

            def store(h):
                sp.wait_ge(out_done, h + 1)
                sp.dma_start(out[h], x_s[:, 2 * TC * h:2 * TC * (h + 1), :]).then_inc(stored, 16)

            write({"PROJ": lambda b, u: rows(b), "ROUTE": lambda b, u: max_rows(b),
                   "WEIGHTS": lambda c, u: weights(c), "STORE": lambda h, u: store(h)})
            sp.wait_ge(stored, 16 * NHALF)

        @block.tensor
        def _(pe):
            readers = {"M0": [], "M1": []}

            def take(name, *read_by):
                for s, value in readers[name]:
                    pe.wait_ge(s, value)
                readers[name] = list(read_by)

            def warm_up(products):
                for _ in range(products):
                    pe.matmul(SQ[0][:, :], zero[:, 0:P], zero[:, :], start=True, stop=True)

            def proj(b, u):
                if b == 0:
                    pe.wait_ge(init_v, 1)
                    warm_up(WARM_LOAD)
                    pe.wait_ge(ld["wqkv"], 16)
                pe.wait_ge(ld_xT[b], 16)
                take("M0", (parts_done, 2 * b + 1))
                take("M1", (vT_done, b + 1), (parts_done, 2 * (b + 1)))
                xT = xT_s[:, b % 2]
                for dst, w0 in ((M0[:, 0:T], 0), (M0[:, T:2 * T], P), (M1[:, 0:T], 2 * P)):
                    for c in range(DC):
                        last = pe.matmul(dst, wqkv_s[:, c, w0:w0 + P], xT[:, c, :], start=(c == 0), stop=(c == DC - 1))
                last.then_inc(proj_done, 1)

            def turn_v(b, u):
                pe.wait_ge(vT_done, b + 1)
                if b == 0:
                    pe.wait_ge(ld["ident"], 16)
                take("M1", (v_done, b + 1))
                for t in range(TC):
                    last = pe.transpose(M1[:, t * 64:(t + 1) * 64], vT[:, t * P:(t + 1) * P], ident[0:64, 0:64])
                last.then_inc(vt_done, 1)

            def mx(b, u):
                i = b % 2
                n = SU * b + u
                if u == 0:
                    if b == 0:
                        warm_up(WARM_ROWS)
                    pe.wait_ge(qk_rows[i], ROWS * (b // 2 + 1))
                    if b >= 2:
                        pe.wait_ge(m_zero, 16 * (b - 1))
                    if b == 0:
                        pe.wait_ge(ld["mask"], 16)
                        pe.wait_ge(ld["identb"], 16)
                if n >= 2:
                    pe.wait_ge(max_done, n - 1)
                o = SQ[n % 2]
                if u < 8:
                    pe.matmul(o[:, :], identb[:], mask[:, :, :], start=True, stop=False, skip_group_check=True)
                    for h in range(4):
                        last = pe.matmul(o[:, h * P:(h + 1) * P], QT[i][:, 4 * u + h, 0:P], KT[i][:, u, 0:P],
                                         start=False, stop=True, skip_group_check=True)
                else:
                    h0 = 2 * (u - 8)
                    ov = o[:, :].rearrange("p (h k) -> p h k", h=2)
                    pe.matmul(ov[:, :, P:T], identb[:], mask[:, 0:2, :], start=True, stop=False,
                              skip_group_check=True)
                    for h in range(2):
                        last = pe.matmul(ov[:, h, :], QT[i][:, h0 + h, P:T], KT[i][:, h0 // REP, :],
                                         start=False, stop=True, skip_group_check=True)
                last.then_inc(sq_done, 1)

            def route(b, u):
                pe.wait_ge(mparts_done, b + 1)
                take("M0", (mrow_done, b + 1))
                for q in range(TC):
                    last = pe.transpose(M0b[0:3 * NH, q * P:(q + 1) * P],
                                        part_m[:, q, :, :].rearrange("p a h -> p (a h)"), identb[:])
                last.then_inc(mT_done, 1)

            TILES = ((0, 0), (0, 1), (1, 1))

            def at(b, u):
                i = b % 2
                g, (kc, q) = u // 3, TILES[u % 3]
                n = SU * b + u
                if u == 0:
                    pe.wait_ge(m_rows, 16 * (b + 1))
                    if b == 0:
                        pe.wait_ge(ones_rows, 32)
                if n >= 2:
                    pe.wait_ge(exp_done, n - 1)
                pe.matmul(ST[n % 2][:, :], KT[i][:, g, kc * P:(kc + 1) * P],
                          QT[i][:, REP * g:REP * (g + 1), q * P:(q + 1) * P], start=True, stop=True).then_inc(st_done, 1)

            def times_v(b, u):
                quad, k3 = divmod(u, 3)
                kc, q = TILES[k3]
                n = 2 * b + quad
                pe.wait_ge(exp_done, 12 * n + 10 + k3)
                if k3 != 1:
                    pe.wait_ge(causal_done, 8 * n + (7, 0, 8)[k3])
                if k3 == 0:
                    pe.wait_ge(v_done, b + 1)
                    if n >= 1:
                        pe.wait_ge(oT_done, n)
                for j in range(4):
                    g = 4 * quad + j
                    last = pe.matmul(PV[q][32 * j:32 * (j + 1), :], V[b % 2][:, kc, g, :],
                                     probs[:, (8 * b + g) % RING, k3, :],
                                     start=(k3 < 2), stop=(k3 != 1), skip_group_check=True)
                if k3 == 2:
                    last.then_inc(pv_done, 1)

            def turn(b, quad):
                pe.wait_ge(oT_done, 2 * b + quad + 1)
                for q in range(TC):
                    take(("M0", "M1")[q], (y_done, 4 * b + 2 * quad + q + 1))
                    for h in range(REP):
                        last = pe.transpose((M0, M1)[q][:, h * P:(h + 1) * P], oT[:, quad, q, h * P:(h + 1) * P], ident[:])
                    last.then_inc(ot_done, 1)

            def flip(src):
                for c in range(DC):
                    for q in range(TC):
                        last = pe.transpose(M0[:, c * T + q * P:c * T + (q + 1) * P], src[:, q, c * P:(c + 1) * P], ident[:])
                return last

            def times(lhsT, rhs):
                for q in range(TC):
                    for c in range(DC):
                        last = pe.matmul(M1[:, q * D:(q + 1) * D], lhsT[:, c, q * P:(q + 1) * P], rhs[:, c, :],
                                         start=(c == 0), stop=(c == DC - 1))
                return last

            def flip_y(b, u):
                pe.wait_ge(y_done, 4 * (b + 1))
                take("M0", (yT_done, b + 1))
                flip(y).then_inc(yt_done, 1)

            def wo(b, u):
                pe.wait_ge(yT_done, b + 1)
                if b == 0:
                    pe.wait_ge(ld["wo"], 16)
                take("M1", (res1_done, b + 1))
                times(yT, wo_s).then_inc(wo_done, 1)

            def flip_x1(b, u):
                pe.wait_ge(x1_done, b + 1)
                take("M0", (x1T_done, b + 1))
                flip(x1).then_inc(x1t_done, 1)

            def xm(b, u):
                pe.wait_ge(x1T_done, b + 1)
                pe.wait_ge(attT_done, b + 1)
                take("M1", (res2_done, b + 1))
                times(x1T, attT[b % 2]).then_inc(xm_done, 1)

            def flip_x2(b, u):
                pe.wait_ge(x2_done, b + 1)
                take("M0", (x2hi_done, b + 1), (x2lo_done, b + 1))
                flip(x2[:, b * TC:(b + 1) * TC, :]).then_inc(x2t_done, 1)

            def logits(b, u):
                pe.wait_ge(x2hi_done, b + 1)
                pe.wait_ge(x2lo_done, b + 1)
                if b == 0:
                    pe.wait_ge(wr_done, 2)
                take("M1", (lsub_done, b + 1))
                for q in range(TC):
                    tok = slice(b * T + q * P, b * T + (q + 1) * P)
                    n = 0
                    for xs, ws in ((x2T_hi, wr_hi), (x2T_hi, wr_lo), (x2T_lo, wr_hi)):
                        for c in range(DC):
                            last = pe.matmul(M1[:, q * E:(q + 1) * E], xs[:, c, tok], ws[:, c, :],
                                             start=(n == 0), stop=(n == 5))
                            n += 1
                last.then_inc(lg_done, 1)

            def turn_gate(b, u):
                pe.wait_ge(gparts_done, b + 1)
                take("M0", (gateT_done, b + 1))
                for q in range(TC):
                    last = pe.transpose(M0b[0:3 * NW, q * P:(q + 1) * P],
                                        part_g[:, q, :, :].rearrange("p a e -> p (a e)"), identb[:])
                last.then_inc(gT_done, 1)

            def xa_qk(b, u):
                pe.wait_ge(ld_ctxT[b], 16)
                if b == 0:
                    pe.wait_ge(ld["xaw"], 16)
                take("M0", (xqk_sb, 2 * (b + 1)))
                for j in range(2):
                    last = pe.matmul(M0[:, j * T:(j + 1) * T], xaw_s[:, j, :], ctxT_s[:, b % 2, :], start=True, stop=True)
                last.then_inc(xqk_done, 1)

            def xa_energy(b, u):
                pe.wait_ge(xqk_sb, 2 * (b + 1))
                take("M1", (xexp_done, 2 * (b + 1)))
                for r in range(TC):
                    last = pe.matmul(M1[:, r * T:(r + 1) * T], xaqk[:, 0, r * P:(r + 1) * P], xaqk[:, 1, :],
                                     start=True, stop=True)
                last.then_inc(xen_done, 1)

            def xa_flip(b, u):
                pe.wait_ge(xatt_done, 2 * (b + 1))
                take("M0", (attT_done, b + 1))
                flip(xae).then_inc(xat_done, 1)

            def open_sums(h, u):
                if h == 0:
                    pe.wait_ge(exp_done, SU * B)
                else:
                    pe.wait_ge(hid_done, EARLY)
                for k in range(2 * h, 2 * h + 2):
                    pe.matmul(bank[k][:, :], zero[:, 0:P], zero[:, :], start=True, stop=False, skip_group_check=True)

            def gate_up(n, j):
                c, half = STEP[n]
                fn = FN[c]
                tok = slice(half * HALF, (half + 1) * HALF)
                if j == 0:
                    if half == 0:
                        pe.wait_ge(whi_done, c + 1)
                        pe.wait_ge(wlo_done, c + 1)
                    if n == 0:
                        pe.wait_ge(oT_done, 2 * B)
                    if n == 1:
                        pe.wait_ge(max_done, SU * B)
                    if n == EARLY:
                        pe.wait_ge(x2hi_done, B)
                        pe.wait_ge(x2lo_done, B)
                    if n == EARLY + 1:
                        for name in readers:
                            take(name)
                    if n >= 2:
                        pe.wait_ge(hid_done, n - 1)
                k = 0
                for ws, xs in ((w_hi, x2T_hi), (w_hi, x2T_lo), (w_lo, x2T_hi)):
                    for d in range(DC):
                        col = (j * DC + d) * P
                        last = pe.matmul(GU[n][j][0:fn, :], ws[c % WRING][:, col:col + fn], xs[:, d, tok],
                                         start=(k == 0), stop=(k == 5))
                        k += 1
                last.then_inc(gu_done, 1)

            def spread(n, u):
                c, half = STEP[n]
                fn = FN[c]
                if n == 0:
                    pe.wait_ge(ld["sel"], 16)
                    pe.wait_ge(gateT_done, B // 2)
                if n == EARLY:
                    pe.wait_ge(gateT_done, B)
                pe.wait_ge(silu_done, n + 1)
                pe.matmul(GU[n][0][0:fn, :], sel[:, c * P:c * P + fn],
                          gateT[:, half * HALF:(half + 1) * HALF], start=True, stop=True).then_inc(spread_done, 1)

            def down(n, u):
                c, half = STEP[n]
                fn = FN[c]
                pe.wait_ge(hhi_done, n + 1)
                pe.wait_ge(hlo_done, n + 1)
                for t4 in range(HALF // P):
                    t = half * (HALF // P) + t4
                    for hs, ws in ((h_hi, w_hi), (h_hi, w_lo), (h_lo, w_hi)):
                        last = pe.matmul(bank[t // 2][:, (t % 2) * D:(t % 2 + 1) * D], hs[n % 2][0:fn, t4 * P:(t4 + 1) * P],
                                         ws[c % WRING][0:fn, GUW:WW],
                                         start=False, stop=False, skip_group_check=True)
                    if c == NCH - 1 and t4 == 1:
                        last.then_inc(sums_done, 1)
                last.then_inc(down_done, 1)

            write({"proj": proj, "turn_v": turn_v, "mx": mx, "route": route, "at": at, "times_v": times_v, "turn": turn,
                   "flip_y": flip_y, "wo": wo, "flip_x1": flip_x1, "xm": xm, "flip_x2": flip_x2, "logits": logits,
                   "turn_gate": turn_gate, "xa_qk": xa_qk, "xa_energy": xa_energy, "xa_flip": xa_flip,
                   "open": open_sums, "gate_up": gate_up, "spread": spread, "down": down})

        @block.scalar
        def _(act):
            def copy(dst, src):
                return nc.scalar.activation(dst, src, ACT.Copy)

            def proj(b, u):
                act.wait_ge(proj_done, b + 1)
                if b >= 1:
                    act.wait_ge(qk_rows[(b - 1) % 2], ROWS * ((b - 1) // 2 + 1))
                copy(part_q[:, 0, :], M0[:, :]).then_inc(hi_done, 1)
                copy(part_k[64:, 0, :], M1[64:, 0:T]).then_inc(hi_done, 1)
                if b >= 1:
                    act.wait_ge(vt_done, b)
                copy(vT[:], M1[0:64, 0:T]).then_inc(vT_done, 1)

            def turn_v(b, u):
                act.wait_ge(vt_done, b + 1)
                if b == 0:
                    act.wait_ge(init_v, 4)
                if b >= 2:
                    act.wait_ge(pv_done, 2 * (b - 1))
                copy(V[b % 2][:, :, :, 0:HD],
                     M1[:, 0:TC * 64].rearrange("p (t g d) -> p t g d", t=TC, g=NKV)).then_inc(v_done, 1)

            def route(b, u):
                act.wait_ge(mT_done, b + 1)
                if b >= 1:
                    act.wait_ge(m_rows, 16 * b)
                copy(mrow[:], M0b[0:3 * NH, 0:T]).then_inc(mrow_done, 1)

            def at(b, u):
                g, k = u // 3, u % 3
                n = SU * b + u
                slot = 8 * b + g
                if k == 0 and slot >= RING:
                    act.wait_ge(pv_done, (slot - RING) // 4 + 1)
                act.wait_ge(st_done, n + 1)
                nc.scalar.activation(probs[:, slot % RING, k, :], ST[n % 2][:, :], ACT.Exp,
                                     scale=SCALE).then_inc(exp_done, 1)

            def take_out(b, quad):
                act.wait_ge(pv_done, 2 * b + quad + 1)
                if b >= 1:
                    act.wait_ge(ot_done, 4 * b - 2 + 2 * quad)
                copy(oT[:, quad, 0, :], PV[0][:, :])
                copy(oT[:, quad, 1, :], PV[1][:, :]).then_inc(oT_done, 1)

            def flip_y(b, u):
                act.wait_ge(yt_done, b + 1)
                if b >= 1:
                    act.wait_ge(wo_done, b)
                copy(yT[:, :, :].rearrange("p c t -> p (c t)"), M0[:, :]).then_inc(yT_done, 1)

            def flip_x1(b, u):
                act.wait_ge(x1t_done, b + 1)
                if b >= 1:
                    act.wait_ge(xm_done, b)
                copy(x1T[:, :, :].rearrange("p c t -> p (c t)"), M0[:, :]).then_inc(x1T_done, 1)

            def flip_x2(b, u):
                act.wait_ge(x2t_done, b + 1)
                copy(x2T_hi[:, :, b * T:(b + 1) * T], M0[:, :].rearrange("p (c t) -> p c t", c=DC)).then_inc(x2hi_done, 1)

            def logits(b, u):
                act.wait_ge(lsub_done, b + 1)
                nc.scalar.activation(lexp[:], lsub[:], ACT.Exp).then_inc(lexp_done, 1)

            def turn_gate(b, u):
                act.wait_ge(gT_done, b + 1)
                copy(gateT[:, b * T:(b + 1) * T], M0b[0:3 * NW, 0:T]).then_inc(gateT_done, 1)

            def xa_energy(b, u):
                act.wait_ge(xmax_done, b + 1)
                if b >= 1:
                    act.wait_ge(xat_done, b)
                for r in range(TC):
                    nc.scalar.activation(xae[:, r, :], M1[:, r * T:(r + 1) * T], ACT.Exp, bias=xam[:, r:r + 1],
                                         accum_out=xal[:, r:r + 1]).then_inc(xexp_done, 1)

            def xa_flip(b, u):
                act.wait_ge(xat_done, b + 1)
                if b >= 2:
                    act.wait_ge(xm_done, b - 1)
                copy(attT[b % 2][:, :, :].rearrange("p c t -> p (c t)"), M0[:, :]).then_inc(attT_done, 1)

            def silu(n, u):
                fn = FN[STEP[n][0]]
                act.wait_ge(gu_done, 2 * n + 1)
                if n == 0:
                    act.wait_ge(pv_done, 2 * B)
                if n >= 2:
                    act.wait_ge(prod_done, n - 1)
                nc.scalar.activation(sg[n % 2][0:fn, :], GU[n][0][0:fn, :], ACT.Silu).then_inc(silu_done, 1)

            def hidden_hi(n, u):
                fn = FN[STEP[n][0]]
                act.wait_ge(hid_done, n + 1)
                if n >= 2:
                    act.wait_ge(down_done, n - 1)
                copy(h_hi[n % 2][0:fn, :], hid[n % 2][0:fn, :]).then_inc(hhi_done, 1)

            write({"PROJ": proj, "TURN_V": turn_v, "ROUTE": route, "at": at, "TIMES_V": take_out, "FLIP_Y": flip_y,
                   "FLIP_X1": flip_x1, "FLIP_X2": flip_x2, "LOGITS": logits, "TURN_GATE": turn_gate,
                   "XA_ENERGY": xa_energy, "XA_FLIP": xa_flip, "SILU": silu, "HID_HI": hidden_hi})

        @block.vector
        def _(v):
            ve = nc.vector
            own = [0]

            def step(ins):
                own[0] += 1
                return ins.then_inc(dve, 1)

            def settle():
                v.wait_ge(dve, own[0])

            ve.memset(zero[:], 0.0).then_inc(init_v, 1)
            ve.memset(QT[0][:, :, :].rearrange("p a b -> p (a b)").bitcast(F32), 0.0).then_inc(init_qt, 1)
            ve.memset(mhalf[:], -0.5).then_inc(init_v, 1)
            for i in range(2):
                step(ve.memset(V[i][:], 0.0))
            settle()
            for i in range(2):
                ve.memset(V[i][:, :, :, HD:HD + 1], 1.0).then_inc(init_v, 1)
            ve.memset(gatew[:, :, E:NW], 1.0).then_inc(init_v, 1)

            def proj(b, u):
                v.wait_ge(hi_done, 2 * (b + 1))
                if b >= 1:
                    v.wait_ge(parts_done, 2 * b)
                step(ve.tensor_tensor(rest_q, M0[:, :], part_q[:, 0, :], ALU.subtract))
                v.wait_ge(vT_done, b + 1)
                step(ve.tensor_tensor(rest_k[64:, :], M1[64:, 0:T], part_k[64:, 0, :], ALU.subtract))
                settle()
                ve.tensor_copy(part_q[:, 1, :], rest_q).then_inc(mid_done, 1)
                ve.tensor_copy(part_k[64:, 1, :], rest_k[64:, :]).then_inc(mid_done, 1)
                v.wait_ge(mid_done, 2 * (b + 1))
                ve.tensor_tensor(part_q[:, 2, :], rest_q, part_q[:, 1, :], ALU.subtract).then_inc(parts_done, 1)
                ve.tensor_tensor(part_k[64:, 2, :], rest_k[64:, :], part_k[64:, 1, :], ALU.subtract).then_inc(parts_done, 1)
                v.wait_ge(parts_done, 2 * (b + 1))

            def mx(b, u):
                n = SU * b + u
                v.wait_ge(sq_done, n + 1)
                if u < 8:
                    o, src = negmax[:, 0, 4 * u:4 * u + 4], SQ[n % 2][:, :].rearrange("p (h k) -> p h k", h=4)
                else:
                    h0 = 2 * (u - 8)
                    o, src = negmax[:, 1, h0:h0 + 2], SQ[n % 2][:, :].rearrange("p (h k) -> p h k", h=2)
                ve.tensor_reduce(o, src, AX_X, ALU.max, negate=True).then_inc(max_done, 1)

            def max_parts(b, u):
                v.wait_ge(max_done, SU * (b + 1))
                if b >= 1:
                    v.wait_ge(mT_done, b)
                    v.wait_ge(mparts_done, b)
                step(ve.tensor_copy(part_m[:, :, 0, :], negmax[:]))
                settle()
                step(ve.tensor_tensor(rest_m[:], negmax[:], part_m[:, :, 0, :], ALU.subtract))
                settle()
                step(ve.tensor_copy(part_m[:, :, 1, :], rest_m[:]))
                settle()
                ve.tensor_tensor(part_m[:, :, 2, :], rest_m[:], part_m[:, :, 1, :], ALU.subtract).then_inc(mparts_done, 1)

            def normalise(b, quad):
                for q in range(TC):
                    n = 4 * b + 2 * quad + q
                    v.wait_ge(ot_done, n + 1)
                    m = (M0, M1)[q][:, :].rearrange("p (h j c) -> p h j c", h=REP, j=4)
                    if n:
                        v.wait_ge(y_done, n)
                    step(ve.reciprocal(rden[:, :].rearrange("p (h j) -> p h j", h=REP), m[:, :, :, HD]))
                    settle()
                    if b >= 1:
                        v.wait_ge(yt_done, b)
                    o = y[:, q, quad * P:(quad + 1) * P].rearrange("p (j h d) -> p h j d", j=4, h=REP)
                    den = rden[:, :].rearrange("p (h j o) -> p h j o", h=REP, o=1).to_broadcast([P, REP, 4, HD])
                    ve.tensor_tensor(o, m[:, :, :, 0:HD], den, ALU.mult).then_inc(y_done, 1)

            norms = [0]

            def statistics(src, tiles):
                for q in range(tiles):
                    step(ve.bn_stats(stat[:, q, :], src[:, q, :]))
                settle()
                for q in range(tiles):
                    step(ve.bn_aggr(mv[:, q, :], stat[:, q, :]))
                settle()
                ve.tensor_scalar(veps[:, 0:tiles], mv[:, 0:tiles, 1], EPS, None, ALU.add).then_inc(var_done, 1)
                norms[0] += 1

            def apply_norm(dst, src, tiles, done, value):
                v.wait_ge(rstd_done, norms[0])
                for q in range(tiles):
                    last = ve.tensor_scalar(dst[:, q, :], src[:, q, :], mv[:, q, 0:1], rstd[:, q:q + 1],
                                            ALU.subtract, ALU.mult)
                    if q < tiles - 1:
                        step(last)
                last.then_inc(done, 1)
                settle()
                v.wait_ge(done, value)

            def residual(dst, m, x, done):
                ve.tensor_tensor(dst[:, :, :].rearrange("p q d -> p (q d)"), m,
                                 x.rearrange("p q d -> p (q d)"), ALU.add).then_inc(done, 1)

            def norm1(b, part):
                if part == 0:
                    if b == 0:
                        v.wait_ge(ld["x"], 16)
                    v.wait_ge(wo_done, b + 1)
                    residual(res, M1[:, :], x_s[:, b * TC:(b + 1) * TC, :], res1_done)
                    v.wait_ge(res1_done, b + 1)
                    statistics(res, TC)
                else:
                    if b >= 1:
                        v.wait_ge(x1t_done, b)
                    apply_norm(x1, res, TC, x1_done, b + 1)

            def norm2(b, part):
                if part == 0:
                    v.wait_ge(xm_done, b + 1)
                    residual(res, M1[:, :], x1[:, :, :], res2_done)
                    v.wait_ge(res2_done, b + 1)
                    statistics(res, TC)
                else:
                    apply_norm(x2[:, b * TC:(b + 1) * TC, :], res, TC, x2_done, b + 1)

            def flip_x2(b, u):
                v.wait_ge(x2hi_done, b + 1)
                ve.tensor_tensor(x2T_lo[:, :, b * T:(b + 1) * T], M0[:, :].rearrange("p (c t) -> p c t", c=DC),
                                 x2T_hi[:, :, b * T:(b + 1) * T].bitcast(F32), ALU.subtract).then_inc(x2lo_done, 1)

            def per_tile(a):
                return a[:, :].rearrange("p (q o) -> p q o", o=1).to_broadcast([P, TC, E])

            def router(b, u):
                v.wait_ge(lg_done, b + 1)
                logits = M1[:, 0:TC * E].rearrange("p (q e) -> p q e", q=TC)
                step(ve.tensor_reduce(lmax[:], logits, AX_X, ALU.max))
                settle()
                ve.tensor_tensor(lsub[:], logits, per_tile(lmax), ALU.subtract).then_inc(lsub_done, 1)

            def score_ranks(b, u):
                v.wait_ge(lexp_done, b + 1)
                step(ve.tensor_reduce(lsum[:], lexp[:], AX_X, ALU.add))
                settle()
                step(ve.reciprocal(lsum[:], lsum[:]))
                settle()
                step(ve.tensor_tensor(score[:], lexp[:], per_tile(lsum), ALU.mult))
                settle()
                if b == 0:
                    v.wait_ge(ld["lower"], 16)
                for q in range(TC):
                    mine = score[:, q, :].rearrange("p (e o) -> p e o", o=1).to_broadcast([P, E, E])
                    other = score[:, q, :].rearrange("p (o j) -> p o j", o=1).to_broadcast([P, E, E])
                    step(ve.tensor_tensor(above[:, q], other, mine, ALU.is_gt))
                    step(ve.tensor_tensor(equal[:, q], other, mine, ALU.is_equal))
                settle()

            def gates(b, u):
                for q in range(TC):
                    step(ve.tensor_tensor(equal[:, q], equal[:, q], lower[:], ALU.mult))
                settle()
                step(ve.tensor_tensor(above[:], above[:], equal[:], ALU.add))
                settle()
                step(ve.tensor_reduce(rank[:], above[:], AX_X, ALU.add))
                settle()
                step(ve.scalar_tensor_tensor(gatew[:, :, 0:E], rank[:], 2.0, score[:], ALU.is_lt, ALU.mult))
                settle()
                if b >= 1:
                    v.wait_ge(gT_done, b)
                    v.wait_ge(gparts_done, b)
                if b == 0:
                    v.wait_ge(init_v, 5)
                step(ve.tensor_copy(part_g[:, :, 0, :], gatew[:]))
                settle()
                step(ve.tensor_tensor(rest_g[:], gatew[:], part_g[:, :, 0, :], ALU.subtract))
                settle()
                step(ve.tensor_copy(part_g[:, :, 1, :], rest_g[:]))
                settle()
                ve.tensor_tensor(part_g[:, :, 2, :], rest_g[:], part_g[:, :, 1, :], ALU.subtract).then_inc(gparts_done, 1)

            def xa_qk(b, u):
                if b == 0:
                    v.wait_ge(ld["wr"], 16)
                    ve.tensor_copy(wr_hi[:], wr_s[:]).then_inc(wr_done, 1)
                    v.wait_ge(wr_done, 1)
                    ve.tensor_tensor(wr_lo[:], wr_s[:], wr_hi[:].bitcast(F32), ALU.subtract).then_inc(wr_done, 1)
                    v.wait_ge(ld["xab"], 16)
                v.wait_ge(xqk_done, b + 1)
                if b >= 1:
                    v.wait_ge(xen_done, b)
                for j in range(2):
                    ve.tensor_scalar(xaqk[:, j, :], M0[:, j * T:(j + 1) * T], xab_s[:, j:j + 1], None,
                                     ALU.add).then_inc(xqk_sb, 1)

            def xa_energy(b, u):
                v.wait_ge(xen_done, b + 1)
                if b >= 1:
                    v.wait_ge(xexp_done, 2 * b)
                    v.wait_ge(xatt_done, 2 * b)
                ve.tensor_reduce(xam[:], M1[:, :].rearrange("p (r k) -> p r k", r=TC), AX_X, ALU.max,
                                 negate=True).then_inc(xmax_done, 1)

            def xa_scale(b, u):
                v.wait_ge(xexp_done, 2 * (b + 1))
                step(ve.reciprocal(xar[:], xal[:]))
                settle()
                for r in range(TC):
                    ve.tensor_scalar(xae[:, r, :], xae[:, r, :], xar[:, r:r + 1], None, ALU.mult).then_inc(xatt_done, 1)

            def weights_hi(c, u):
                v.wait_ge(ld_w[c % 2], 16 * (c // 2 + 1))
                if c == WOWN:
                    v.wait_ge(pv_done, 2 * B)
                if c >= WRING:
                    v.wait_ge(down_done, STEP.index((c - WRING, NHALF - 1)) + 1)
                ve.tensor_copy(w_hi[c % WRING][:], w_in[:, c % 2]).then_inc(whi_done, 1)

            def product(n, u):
                fn = FN[STEP[n][0]]
                v.wait_ge(silu_done, n + 1)
                v.wait_ge(gu_done, 2 * (n + 1))
                if n >= 2:
                    v.wait_ge(hid_done, n - 1)
                ve.tensor_tensor(gu[n % 2][0:fn, :], GU[n][1][0:fn, :], sg[n % 2][0:fn, :], ALU.mult).then_inc(prod_done, 1)

            def hidden(n, u):
                fn = FN[STEP[n][0]]
                v.wait_ge(prod_done, n + 1)
                v.wait_ge(spread_done, n + 1)
                if n >= 2:
                    v.wait_ge(hhi_done, n - 1)
                    v.wait_ge(hlo_done, n - 1)
                ve.tensor_tensor(hid[n % 2][0:fn, :], GU[n][0][0:fn, :], gu[n % 2][0:fn, :], ALU.mult).then_inc(hid_done, 1)

            def last_norm(h, part):
                if part == 0:
                    for k in range(2):
                        if k == 0:
                            v.wait_ge(sums_done, h + 1)
                        else:
                            v.wait_ge(down_done, STEP.index((NCH - 1, h)) + 1)
                        b = 2 * h + k
                        step(ve.tensor_tensor(res_l[:, k * TC:(k + 1) * TC, :].rearrange("p q d -> p (q d)"), bank[b][:, :],
                                              x2[:, b * TC:(b + 1) * TC, :].rearrange("p q d -> p (q d)"), ALU.add))
                        if k == 1:
                            settle()
                    statistics(res_l, 2 * TC)
                else:
                    apply_norm(x_s[:, 2 * TC * h:2 * TC * (h + 1), :], res_l, 2 * TC, out_done, h + 1)

            write({"PROJ": proj, "mx": mx, "MAX_PARTS": max_parts, "TURN": normalise, "NORM1": norm1, "NORM2": norm2,
                   "FLIP_X2": flip_x2, "LOGITS": router, "SCORES": score_ranks, "GATES": gates, "XA_QK": xa_qk, "XA_ENERGY": xa_energy, "XA_SCALE": xa_scale,
                   "WEIGHTS": weights_hi, "PROD": product, "HID": hidden, "LAST_NORM": last_norm})

        @block.gpsimd
        def _(pool):
            gp = nc.gpsimd
            gp.memset(ones[:], 1.0).then_inc(init_p, 1)
            for tile in (KT[0], KT[1], QT[1]):
                gp.memset(tile[:, :, :].rearrange("p a b -> p (a b)").bitcast(F32), 0.0).then_inc(init_p, 1)
            norms = [0]

            def rsqrt(tiles):
                if norms[0] == 0:
                    pool.wait_ge(init_v, 2)
                norms[0] += 1
                pool.wait_ge(var_done, norms[0])
                gp.tensor_tensor(rstd[:, 0:tiles], veps[:, 0:tiles], mhalf[:, 0:tiles], ALU.pow).then_inc(rstd_done, 1)

            def at(b, u):
                if u % 3 == 1:
                    return
                pool.wait_ge(exp_done, SU * b + u + 1)
                t = probs[:, (8 * b + u // 3) % RING, u % 3, :].rearrange("p (h q) -> p h q", h=REP)
                gp.affine_select(out=t, in_=t, compare_op=ALU.is_ge, fill=0.0, base=0,
                                 pattern=[[0, REP], [1, P]], channel_multiplier=-1).then_inc(causal_done, 1)

            def norm(b, part):
                if part == 0:
                    rsqrt(TC)


            def weights_lo(c, u):
                pool.wait_ge(whi_done, c + 1)
                gp.tensor_tensor(w_lo[c % WRING][:], w_in[:, c % 2], w_hi[c % WRING][:].bitcast(F32),
                                 ALU.subtract).then_inc(wlo_done, 1)

            def hidden_lo(n, u):
                fn = FN[STEP[n][0]]
                pool.wait_ge(hhi_done, n + 1)
                if n >= 2:
                    pool.wait_ge(down_done, n - 1)
                gp.tensor_tensor(h_lo[n % 2][0:fn, :], hid[n % 2][0:fn, :], h_hi[n % 2][0:fn, :].bitcast(F32),
                                 ALU.subtract).then_inc(hlo_done, 1)

            def last_norm(h, part):
                if part == 0:
                    rsqrt(2 * TC)

            write({"at": at, "NORM1": norm, "NORM2": norm, "WEIGHTS": weights_lo, "HID_LO": hidden_lo,
                   "LAST_NORM": last_norm})


def constants():
    bf = np.dtype("bfloat16")
    ident = np.eye(P, dtype=np.float32)
    later = np.arange(P)[None, :] > np.arange(P)[:, None]
    mask = np.repeat(np.where(later, MASKED, 0.0)[:, None, :], REP, axis=1).astype(bf)
    sel = np.zeros((3, NW, NCH * P), np.float32)
    for f in range(F):
        sel[:, min(f // FE, E), f] = 1.0
    lower = np.tile(np.tril(np.ones((E, E), np.float32), -1), (P, 1, 1))
    return {"c_ident": ident, "c_identb": ident.astype(bf), "c_mask": mask,
            "c_sel": sel.reshape(3 * NW, NCH * P).astype(bf), "c_lower": lower}


def rows(a, chunks):
    return np.ascontiguousarray(a.reshape(chunks, P, -1).transpose(1, 0, 2))


def kernel(**inputs):
    from concourse import bacc
    from concourse.bass_utils import run_bass_kernel_spmd

    a = {k: np.asarray(v) for k, v in inputs.items()}
    x = a["x"].reshape(B * T, D)
    wq = a["L0_attn_wq"].reshape(D, NH // 2, 2, HD).transpose(0, 2, 3, 1).reshape(D, NH * HD)
    wk = a["L0_attn_wk"].reshape(D, NKV, HD).transpose(0, 2, 1).reshape(D, NKV * HD)
    gate, up = (np.concatenate([a[n].reshape(E * FE, D), a[m]]).T for n, m in (("L0_ffn_Wg", "L0_ffn_Wsg"), ("L0_ffn_Wu", "L0_ffn_Wsu")))
    down = np.concatenate([a["L0_ffn_Wd"].transpose(0, 2, 1).reshape(E * FE, D), a["L0_ffn_Wsd"].T])
    w_ffn = np.zeros((NCH, P, WW), np.float32)
    for c, fn in enumerate(FN):
        f = slice(c * P, c * P + fn)
        for j, w in enumerate((gate, up)):
            for d in range(DC):
                w_ffn[c, :, (j * DC + d) * P:(j * DC + d) * P + fn] = w[d * P:(d + 1) * P, f]
        w_ffn[c, :fn, GUW:] = down[f]
    arrays = {
        "x_tok": rows(x, B * TC),
        "x_T": rows(np.ascontiguousarray(x.T), DC),
        "ctx_T": np.ascontiguousarray(a["ctx_1024"].reshape(B * T, CTX).T),
        "w_qkv": rows(np.concatenate([wq, a["L0_attn_wv"], wk], axis=1), DC),
        "w_o": rows(a["L0_attn_wo"], DC),
        "xa_w": np.ascontiguousarray(np.stack([a["L0_xattn_Wq"].T, a["L0_xattn_Wk"].T], axis=1)),
        "xa_b": np.ascontiguousarray(np.stack([a["L0_xattn_bq"], a["L0_xattn_bk"]], axis=1)),
        "w_r": rows(np.ascontiguousarray(a["L0_ffn_Wr"].T), DC),
        "w_ffn": w_ffn,
        **constants(),
    }
    nc = bacc.Bacc("TRN2", target_bir_lowering=False, num_devices=1)
    args = [nc.dram_tensor(n, v.shape, mybir.dt.from_np(v.dtype), kind="ExternalInput").ap() for n, v in arrays.items()]
    out = nc.dram_tensor("out", (NHALF, P, HALF // P, D), F32, kind="ExternalOutput").ap()
    build_layer(nc, *args, out)
    r = run_bass_kernel_spmd(nc, [arrays], core_ids=[0])
    return np.asarray(r.results[0]["out"]).transpose(0, 2, 1, 3).reshape(B, T, D)
```

```python
from contextlib import ExitStack

import numpy as np

import concourse.bass as bass
from concourse import mybir

F32 = mybir.dt.float32
F32R = mybir.dt.float32r
BF16 = mybir.dt.bfloat16
ACT = mybir.ActivationFunctionType
ALU = mybir.AluOpType
AX_X = mybir.AxisListType.X

P = 128
B, T, D = 4, 256, 256
TC = T // P
DC = D // P
NH, NKV, HD = 32, 8, 8
REP = NH // NKV
CTX = 128
E, FE, FS = 8, 176, 352
F = E * FE + FS
NCH = -(-F // P)
FN = [min(P, F - c * P) for c in range(NCH)]
HALF = 512
NHALF = B * T // HALF
WRING = 6
WOWN = 3
EPS = 1e-5
MASKED = -3e38
SCALE = float(HD) ** -0.5
COMBOS = [(0, 0), (0, 1), (1, 0), (1, 1), (0, 2), (2, 0)]
MROW = len(COMBOS) * HD
GUW = 2 * DC * P
WW = GUW + D
NW = E + 1
RING = 6
WARM_LOAD, WARM_ROWS = 8, 14
SU = 24


EARLY = WRING
LATE = 3
STEP = [(c, h) for h in range(NHALF) for c in range(EARLY)]
STEP += [(c, h) for c in range(EARLY, NCH - LATE) for h in range(NHALF)]
STEP += [(c, h) for h in range(NHALF) for c in range(NCH - LATE, NCH)]
STEPS = len(STEP)


MX = [(-6.41, 0.807), (7.32, 0.501), (5.33, 0.577)]
START = [
    (-7.69, "PROJ", 0, 0), (-7.56, "proj", 0, 0), (-4.95, "turn_v", 0, 0), (8.63, "TURN_V", 0, 0),
    (33.55, "proj", 1, 0), (45.36, "PROJ", 1, 0), (78.17, "MAX_PARTS", 0, 0), (93.54, "ROUTE", 0, 0),
    (94.65, "route", 0, 0),
]
BODY_0 = [
    (12.35, "MAX_PARTS", 1, 0), (12.94, "xa_qk", 0, 0), (15.5, "XA_QK", 0, 0), (15.53, "times_v", 0, 0),
    (15.87, "xa_energy", 0, 0), (17.14, "XA_ENERGY", 0, 0), (17.15, "times_v", 0, 1), (17.43, "route", 1, 0),
    (17.86, "ROUTE", 1, 0), (18.3, "TIMES_V", 0, 0), (18.95, "times_v", 0, 2), (19.76, "turn_v", 1, 0),
    (20.66, "xa_flip", 0, 0), (20.76, "TURN_V", 1, 0), (21.46, "XA_SCALE", 0, 0), (21.65, "XA_FLIP", 0, 0),
    (22.65, "PROJ", 2, 0), (26.34, "proj", 2, 0), (38.56, "WEIGHTS", 0, 0),
]
BODY_1 = [
    (-5.81, "times_v", -1, 3), (-5.39, "times_v", -1, 4), (1.69, "turn", -1, 0), (4.45, "TURN", -1, 0),
    (5.41, "times_v", -1, 5), (5.63, "turn", -1, 1), (5.85, "TIMES_V", -1, 1), (6.52, "TURN", -1, 1),
    (7.51, "TURN_GATE", -2, 0), (8.9, "turn_gate", -2, 0), (9.18, "flip_y", -1, 0), (9.75, "FLIP_Y", -1, 0),
    (10.31, "wo", -1, 0), (11.02, "NORM1", -1, 0), (11.04, "times_v", 0, 0), (12.06, "xa_qk", 0, 0),
    (12.17, "XA_QK", 0, 0), (12.22, "times_v", 0, 1), (13.44, "NORM1", -1, 1), (14.68, "xa_energy", 0, 0),
    (16.63, "flip_x1", -1, 0), (16.94, "FLIP_X1", -1, 0), (17.13, "XA_ENERGY", 0, 0), (17.85, "XA_SCALE", 0, 0),
    (18.28, "TIMES_V", 0, 0), (18.34, "times_v", 0, 2), (18.95, "xm", -1, 0), (19.02, "NORM2", -1, 0),
    (21.19, "XA_FLIP", 0, 0), (21.26, "turn_v", 1, 0), (21.3, "xa_flip", 0, 0), (21.43, "TURN_V", 1, 0),
    (21.82, "MAX_PARTS", 1, 0), (22.02, "NORM2", -1, 1), (22.31, "route", 1, 0), (22.86, "ROUTE", 1, 0),
    (23.03, "PROJ", 2, 0), (23.34, "proj", 2, 0), (24.51, "WEIGHTS", 0, 0), (26.35, "FLIP_X2", -1, 0),
    (27.17, "flip_x2", -1, 0), (27.94, "LOGITS", -1, 0), (29.35, "SCORES", -1, 0), (29.93, "logits", -1, 0),
    (31.58, "GATES", -1, 0),
]
BODY_2 = [
    (-11.65, "times_v", -1, 3), (-0.31, "times_v", -1, 4), (1.81, "turn", -1, 0), (1.82, "TURN", -1, 0),
    (2.35, "TURN_GATE", -2, 0), (3.34, "turn_gate", -2, 0), (3.73, "times_v", -1, 5), (5.71, "TIMES_V", -1, 1),
    (6.84, "TURN", -1, 1), (6.99, "turn", -1, 1), (7.63, "FLIP_Y", -1, 0), (8.32, "flip_y", -1, 0),
    (10.78, "wo", -1, 0), (11.43, "NORM1", -1, 0), (11.63, "times_v", 0, 0), (12.79, "xa_qk", 0, 0),
    (12.89, "XA_QK", 0, 0), (13.62, "NORM1", -1, 1), (13.88, "xa_energy", 0, 0), (14.12, "times_v", 0, 1),
    (15.29, "flip_x1", -1, 0), (15.89, "times_v", 0, 2), (16.24, "XA_ENERGY", 0, 0), (17.76, "FLIP_X1", -1, 0),
    (17.9, "TIMES_V", 0, 0), (18.95, "xm", -1, 0), (19.51, "XA_SCALE", 0, 0), (19.52, "NORM2", -1, 0),
    (20.38, "TURN_V", 1, 0), (21.12, "turn_v", 1, 0), (21.16, "MAX_PARTS", 1, 0), (21.48, "XA_FLIP", 0, 0),
    (21.51, "ROUTE", 1, 0), (22.66, "xa_flip", 0, 0), (22.66, "NORM2", -1, 1), (23.01, "PROJ", 2, 0),
    (23.82, "proj", 2, 0), (23.85, "route", 1, 0), (24.5, "WEIGHTS", 0, 0), (24.67, "FLIP_X2", -1, 0),
    (26.03, "LOGITS", -1, 0), (26.33, "SCORES", -1, 0), (33.55, "GATES", -1, 0), (36.76, "flip_x2", -1, 0),
    (37.6, "logits", -1, 0),
]
BODY_3 = [
    (-0.91, "TURN", -1, 0), (0.2, "times_v", -1, 3), (0.98, "times_v", -1, 4), (1.59, "TURN_GATE", -2, 0),
    (2.89, "turn_gate", -2, 0), (3.18, "times_v", -1, 5), (3.61, "turn", -1, 0), (3.74, "TIMES_V", -1, 1),
    (5.63, "turn", -1, 1), (7.48, "FLIP_Y", -1, 0), (7.81, "flip_y", -1, 0), (9.15, "wo", -1, 0),
    (11.65, "xa_qk", 0, 0), (12.9, "TURN", -1, 1), (13.02, "times_v", 0, 0), (14.26, "XA_QK", 0, 0),
    (14.59, "NORM1", -1, 0), (15.76, "XA_ENERGY", 0, 0), (15.99, "xa_energy", 0, 0), (16.8, "times_v", 0, 1),
    (17.79, "times_v", 0, 2), (20.08, "NORM1", -1, 1), (20.15, "XA_SCALE", 0, 0), (23.12, "xa_flip", 0, 0),
    (23.4, "XA_FLIP", 0, 0), (23.9, "TIMES_V", 0, 0),
]
BODY = [BODY_0, BODY_1, BODY_2, BODY_3]
FIRST_STEPS = [
    (-16.94, "flip_x1", 2, 0), (-12.9, "TURN", 3, 0), (-10.74, "open", 0, 0), (-9.93, "FLIP_X1", 2, 0),
    (-9.68, "WEIGHTS", 3, 0), (-2.5, "times_v", 3, 3), (-2.39, "TIMES_V", 3, 1), (-1.83, "times_v", 3, 4),
    (-0.94, "TURN", 3, 1), (-0.61, "times_v", 3, 5), (-0.61, "turn", 3, 0), (-0.05, "turn", 3, 1),
    (0.56, "xm", 2, 0), (0.78, "flip_y", 3, 0), (0.82, "NORM2", 2, 0), (1.2, "FLIP_Y", 3, 0), (1.26, "wo", 3, 0),
    (1.34, "NORM2", 2, 1), (1.51, "flip_x2", 2, 0), (1.93, "NORM1", 3, 0), (2.71, "FLIP_X2", 2, 0),
    (3.99, "WEIGHTS", 4, 0), (4.52, "logits", 2, 0), (7.17, "NORM1", 3, 1), (7.18, "LOGITS", 2, 0),
    (7.89, "SCORES", 2, 0), (8.19, "flip_x1", 3, 0), (9.07, "xm", 3, 0), (9.29, "WEIGHTS", 5, 0),
    (10.43, "GATES", 2, 0), (11.24, "FLIP_X1", 3, 0), (11.27, "turn_gate", 2, 0), (11.55, "NORM2", 3, 0),
    (12.55, "NORM2", 3, 1), (13.13, "flip_x2", 3, 0), (13.51, "TURN_GATE", 2, 0), (15.65, "FLIP_X2", 3, 0),
    (16.41, "logits", 3, 0), (16.97, "LOGITS", 3, 0), (17.09, "SCORES", 3, 0), (17.98, "GATES", 3, 0),
    (18.28, "TURN_GATE", 3, 0), (20.45, "turn_gate", 3, 0), (26.52, "open", 1, 0),
]
FFN = [
    (-0, "gate_up", 0, 0), (0.95, "gate_up", 0, 1), (2.64, "SILU", 0, 0), (3.14, "PROD", 0, 0),
    (3.38, "spread", 0, 0), (4.67, "HID", 0, 0), (5.99, "HID_LO", 0, 0), (6.19, "HID_HI", 0, 0),
    (8.87, "down", 0, 0),
]
LAST = [[(9.77, "LAST_NORM", 0, 0), (11.97, "LAST_NORM", 0, 1), (12.35, "STORE", 0, 0), (14.72, "STORE", 1, 0), (16.16, "LAST_NORM", 1, 0), (20.02, "LAST_NORM", 1, 1)],
        [(10.03, "LAST_NORM", 0, 0), (11.17, "LAST_NORM", 1, 0), (12.49, "STORE", 0, 0), (14.15, "STORE", 1, 0), (21.53, "LAST_NORM", 0, 1), (21.95, "LAST_NORM", 1, 1)]]


def program_order():
    placed = []

    def put(base, entries, b=0):
        placed.extend((base + pos, len(placed) + k, name, b + db, u) for k, (pos, name, db, u) in enumerate(entries))

    put(-100, START)
    put(-100, [(50 + u, "mx", 0, u) for u in range(SU)])
    for b in range(B):
        put(100 * b, [(u, "at", b, u) for u in range(SU)])
        if b + 1 < B:
            m0, rate = MX[b]
            put(100 * b, [(m0 + rate * u, "mx", b + 1, u) for u in range(SU)])
        put(100 * b, [e for e in BODY[b] if 0 <= b + e[2] < B], b)
    put(100 * B, FIRST_STEPS)
    for n in range(STEPS):
        put(100 * B + 3 * n, FFN, n)
    for c in range(WRING, NCH):
        put(100 * B + 3 * STEP.index((c - WRING, NHALF - 1)) + 9.5, [(0, "WEIGHTS", c, 0)])
    for h in range(NHALF):
        put(100 * B + 3 * STEP.index((NCH - 1, h)), LAST[h], 2 * h)
    return [x[2:] for x in sorted(placed)]


def build_layer(nc, x_tok, x_T, ctx_T, w_qkv, w_o, xa_w, xa_b, w_r, w_ffn,
                c_ident, c_identb, c_mask, c_sel, c_lower, out):
    with ExitStack() as ctx:
        def sb(name, shape, dt=F32):
            return ctx.enter_context(nc.sbuf_tensor(name, shape, dt))

        def sem(name):
            return ctx.enter_context(nc.semaphore(name))

        ident = sb("ident", [P, P])
        identb = sb("identb", [P, P], BF16)
        mask = sb("mask", [P, REP, P], BF16)
        sel = sb("sel", [3 * NW, NCH * P], BF16)
        lower = sb("lower", [P, E, E])
        wqkv_s = sb("wqkv_s", [P, DC, NH * HD + 2 * NKV * HD])
        wo_s = sb("wo_s", [P, DC, D])
        xaw_s = sb("xaw_s", [P, 2, P])
        xab_s = sb("xab_s", [P, 2])
        wr_s = sb("wr_s", [P, DC, E])
        wr_hi = sb("wr_hi", [P, DC, E], F32R)
        wr_lo = sb("wr_lo", [P, DC, E], F32R)
        x_s = sb("x_s", [P, B * TC, D])
        xT_s = sb("xT_s", [P, 2, DC, T])
        ctxT_s = sb("ctxT_s", [P, 2, T])
        rest_k = sb("rest_k", [P, T])
        vT = sb("vT", [NKV * HD, T])
        part_q = [sb(f"part_q{i}", [P, 3, 2 * T], BF16) for i in range(2)]
        part_k = [sb(f"part_k{i}", [P, 3, T], BF16) for i in range(2)]
        KT = [sb(f"KT{i}", [P, NKV, T], BF16) for i in range(2)]
        V = [sb(f"V{i}", [P, TC, NKV, 32]) for i in range(2)]
        negmax = sb("negmax", [P, TC, NH])
        rest_m = sb("rest_m", [P, TC, NH])
        ones = sb("ones", [3, NKV * T], BF16)
        part_m = sb("part_m", [P, TC, 3, NH], BF16)
        mrow = sb("mrow", [3 * NH, T], BF16)
        oT = sb("oT", [P, 2, TC, 512])
        rden = sb("rden", [P, REP * 4])
        y = sb("y", [P, TC, D])
        yT = sb("yT", [P, DC, T])
        res = sb("res", [P, TC, D])
        rest_q = res[:, :, :].rearrange("p q d -> p (q d)")
        x1 = sb("x1", [P, TC, D])
        x1T = sb("x1T", [P, DC, T])
        stat = sb("stat", [P, 2 * TC, 6])
        mv = sb("mv", [P, 2 * TC, 2])
        veps = sb("veps", [P, 2 * TC])
        rstd = sb("rstd", [P, 2 * TC])
        mhalf = sb("mhalf", [P, 2 * TC])
        xaqk = sb("xaqk", [P, 2, T])
        xam = sb("xam", [P, TC])
        xae = sb("xae", [P, TC, T])
        xal = sb("xal", [P, TC])
        xar = sb("xar", [P, TC])
        attT = [sb(f"attT{i}", [P, TC, T]) for i in range(2)]
        x2 = sb("x2", [P, B * TC, D])
        x2T_hi = sb("x2T_hi", [P, DC, B * T], F32R)
        x2T_lo = sb("x2T_lo", [P, DC, B * T], F32R)
        lmax = sb("lmax", [P, TC])
        lexp = sb("lexp", [P, TC, E])
        lsum = sb("lsum", [P, TC])
        score = sb("score", [P, TC, E])
        above = sb("above", [P, TC, E, E])
        equal = sb("equal", [P, TC, E, E])
        lsub = sb("lsub", [P, TC, E])
        rank = sb("rank", [P, TC, E])
        gatew = sb("gatew", [P, TC, NW])
        rest_g = sb("rest_g", [P, TC, NW])
        part_g = sb("part_g", [P, TC, 3, NW], BF16)
        gateT = sb("gateT", [3 * NW, B * T], BF16)
        w_in = sb("w_in", [P, 2, WW])
        w_hi = [sb(f"w_hi{i}", [P, WW], F32R) for i in range(WOWN)]
        w_lo = [sb(f"w_lo{i}", [P, WW], F32R) for i in range(WOWN)]
        zero = sb("zero", [P, 512], BF16)
        with ExitStack() as attention:
            probs = attention.enter_context(nc.sbuf_tensor("probs", [P, RING, 3, 512], F32))
            QT = [attention.enter_context(nc.sbuf_tensor(f"QT{i}", [P, NH, T], BF16)) for i in range(2)]
        sg = [sb(f"sg{i}", [P, HALF]) for i in range(2)]
        gu = [sb(f"gu{i}", [P, HALF]) for i in range(2)]
        hid = [sb(f"hid{i}", [P, HALF]) for i in range(2)]
        h_hi = [sb(f"h_hi{i}", [P, HALF], F32R) for i in range(2)]
        h_lo = [sb(f"h_lo{i}", [P, HALF], F32R) for i in range(2)]
        res_l = sb("res_l", [P, 2 * TC, D])
        w_hi += [sb(f"w_hi{i}", [P, WW], F32R) for i in range(WOWN, WRING)]
        w_lo += [sb(f"w_lo{i}", [P, WW], F32R) for i in range(WOWN, WRING)]

        bank = [ctx.enter_context(nc.psum_tensor(f"bank{i}", [P, 512], F32)) for i in range(8)]
        ST = bank[0:2]
        SQ = bank[2:4]
        PV = bank[4:6]
        M0, M1 = bank[6:8]
        GU = [(bank[4], bank[5]) if n % 2 == 0 else (bank[2], bank[3]) if n < EARLY else (M0, M1) for n in range(STEPS)]
        M0b = M0[:, :].bitcast(BF16)

        ld = {n: sem(f"ld_{n}") for n in ("ident", "identb", "mask", "sel", "lower", "wqkv", "wo", "xaw", "xab",
                                          "wr", "x")}
        ld_xT = [sem(f"ld_xT{b}") for b in range(B)]
        ld_ctxT = [sem(f"ld_ctxT{b}") for b in range(B)]
        ones_rows = sem("ones_rows")
        ld_w = [sem(f"ld_w{i}") for i in range(2)]
        init_v = sem("init_v")
        init_p = sem("init_p")
        init_qt = sem("init_qt")
        wr_done = sem("wr_done")
        kv_done = sem("kv_done")
        q_done = sem("q_done")
        k_parts = [sem(f"k_{n}") for n in ("hi", "mid", "lo")]
        q_parts = [sem(f"q_{n}") for n in ("hi", "mid", "lo")]
        vT_done = sem("vT_done")
        vt_done = sem("vt_done")
        v_done = sem("v_done")
        qk_rows = [sem(f"qk_rows{i}") for i in range(2)]
        sq_done = sem("sq_done")
        max_done = sem("max_done")
        mparts_done = sem("mparts_done")
        mT_done = sem("mT_done")
        mrow_done = sem("mrow_done")
        m_zero = sem("m_zero")
        m_rows = sem("m_rows")
        st_done = sem("st_done")
        exp_done = sem("exp_done")
        causal_done = sem("causal_done")
        pv_done = sem("pv_done")
        oT_done = sem("oT_done")
        ot_done = sem("ot_done")
        y_done = sem("y_done")
        yt_done = sem("yt_done")
        yT_done = sem("yT_done")
        wo_done = sem("wo_done")
        res1_done = sem("res1_done")
        res2_done = sem("res2_done")
        x1_done = sem("x1_done")
        x1t_done = sem("x1t_done")
        x1T_done = sem("x1T_done")
        xm_done = sem("xm_done")
        x2_done = sem("x2_done")
        x2t_done = sem("x2t_done")
        x2hi_done = sem("x2hi_done")
        x2lo_done = sem("x2lo_done")
        var_done = sem("var_done")
        rstd_done = sem("rstd_done")
        xqk_done = sem("xqk_done")
        xqk_sb = sem("xqk_sb")
        xen_done = sem("xen_done")
        xmax_done = sem("xmax_done")
        xexp_done = sem("xexp_done")
        xatt_done = sem("xatt_done")
        xat_done = sem("xat_done")
        attT_done = sem("attT_done")
        lg_done = sem("lg_done")
        lsub_done = sem("lsub_done")
        lexp_done = sem("lexp_done")
        gparts_done = sem("gparts_done")
        gT_done = sem("gT_done")
        gateT_done = sem("gateT_done")
        dve = sem("dve")
        whi_done = sem("whi_done")
        wlo_done = sem("wlo_done")
        gu_done = sem("gu_done")
        silu_done = sem("silu_done")
        spread_done = sem("spread_done")
        prod_done = sem("prod_done")
        hid_done = sem("hid_done")
        hhi_done = sem("hhi_done")
        hlo_done = sem("hlo_done")
        down_done = sem("down_done")
        sums_done = sem("sums_done")
        out_done = sem("out_done")
        stored = sem("stored")

        order = program_order()

        def write(stages):
            for name, b, u in order:
                if name in stages:
                    stages[name](b, u)

        ROWS = 16 * 2 * len(COMBOS)
        block = ctx.enter_context(nc.Block())

        @block.sync
        def _(sp):
            def load(dst, src, s):
                sp.dma_start(dst, src).then_inc(s, 16)

            def load_xT(b):
                load(xT_s[:, b % 2], x_T[:, :, b * T:(b + 1) * T], ld_xT[b])

            def load_ctxT(b):
                load(ctxT_s[:, b % 2], ctx_T[:, b * T:(b + 1) * T], ld_ctxT[b])

            load(wqkv_s[:], w_qkv, ld["wqkv"])
            load_xT(0)
            load(identb[:], c_identb, ld["identb"])
            load(mask[:], c_mask, ld["mask"])
            load(ident[:], c_ident, ld["ident"])
            load_xT(1)
            load(xaw_s[:], xa_w, ld["xaw"])
            load_ctxT(0)
            load(xab_s[:], xa_b, ld["xab"])
            load_ctxT(1)
            load(wr_s[:], w_r, ld["wr"])

            def rows(b):
                i = b % 2
                if b < 2:
                    sp.wait_ge(init_qt, 1)
                    sp.wait_ge(init_p, b + 2 + (b > 0))
                    sp.dma_start(KT[i][MROW:MROW + 3, :, :], ones[:]).then_inc(ones_rows, 16)
                else:
                    sp.wait_ge(st_done, SU * (b - 1))
                    stale = QT[i][MROW:MROW + 3, :, :].rearrange("p a b -> p (a b)")
                    sp.dma_start(stale.rearrange("p (r n) -> p r n", n=512),
                                 zero[0:3, :].rearrange("p (o n) -> p o n", o=1).to_broadcast([3, NH * T // 512, 512])
                                 ).then_inc(m_zero, 16)
                for rows_of, source, parts, which in ((KT[i], part_k[i][64:], k_parts, 1), (QT[i], part_q[i], q_parts, 0)):
                    for part in range(3):
                        sp.wait_ge(parts[part], b + 1)
                        for c in (c for c, combo in enumerate(COMBOS) if combo[which] == part):
                            sp.dma_start(rows_of[HD * c:HD * (c + 1), :, :], source[:, part, :]).then_inc(qk_rows[i], 16)
                if b == 0:
                    for c in range(2):
                        load(w_in[:, c], w_ffn[c], ld_w[c])
                    load(x_s[:], x_tok, ld["x"])
                    load(wo_s[:], w_o, ld["wo"])
                    load(lower[:], c_lower, ld["lower"])
                    load(sel[:], c_sel, ld["sel"])

            def max_rows(b):
                sp.wait_ge(mrow_done, b + 1)
                sp.dma_start(QT[b % 2][MROW:MROW + 3, :, :], mrow[:]).then_inc(m_rows, 16)
                if b + 2 < B:
                    load_xT(b + 2)
                if 1 <= b < B - 1:
                    sp.wait_ge(xqk_done, b)
                    load_ctxT(b + 1)

            def weights(c):
                if c + 2 < NCH:
                    sp.wait_ge(whi_done, c + 1)
                    sp.wait_ge(wlo_done, c + 1)
                    load(w_in[:, c % 2], w_ffn[c + 2], ld_w[c % 2])

            def store(b):
                sp.wait_ge(out_done, b + 1)
                sp.dma_start(out[b], x_s[:, b * TC:(b + 1) * TC, :]).then_inc(stored, 16)

            write({"PROJ": lambda b, u: rows(b), "ROUTE": lambda b, u: max_rows(b),
                   "WEIGHTS": lambda c, u: weights(c), "STORE": lambda h, u: store(h)})
            sp.wait_ge(stored, 16 * B)

        @block.tensor
        def _(pe):
            readers = {"M0": [], "M1": []}

            def take(name, *read_by):
                for s, value in readers[name]:
                    pe.wait_ge(s, value)
                readers[name] = list(read_by)

            def warm_up(products):
                for _ in range(products):
                    pe.matmul(SQ[0][:, :], zero[:, 0:P], zero[:, :], start=True, stop=True)

            def proj(b, u):
                if b == 0:
                    pe.wait_ge(init_v, 1)
                    warm_up(WARM_LOAD)
                    pe.wait_ge(ld["wqkv"], 16)
                pe.wait_ge(ld_xT[b], 16)
                take("M0", (q_parts[1], b + 1))
                take("M1", (vT_done, b + 1), (k_parts[1], b + 1))
                xT = xT_s[:, b % 2]
                for dst, w0, done in ((M1[:, 0:T], 2 * P, kv_done), (M0[:, 0:T], 0, None), (M0[:, T:2 * T], P, q_done)):
                    for c in range(DC):
                        last = pe.matmul(dst, wqkv_s[:, c, w0:w0 + P], xT[:, c, :], start=(c == 0), stop=(c == DC - 1))
                    if done:
                        last.then_inc(done, 1)

            def turn_v(b, u):
                pe.wait_ge(vT_done, b + 1)
                if b == 0:
                    pe.wait_ge(ld["ident"], 16)
                take("M1", (v_done, b + 1))
                for t in range(TC):
                    last = pe.transpose(M1[:, t * 64:(t + 1) * 64], vT[:, t * P:(t + 1) * P], ident[0:64, 0:64])
                last.then_inc(vt_done, 1)

            def mx(b, u):
                i = b % 2
                n = SU * b + u
                if u == 0:
                    if b == 0:
                        warm_up(WARM_ROWS)
                    pe.wait_ge(qk_rows[i], ROWS * (b // 2 + 1))
                    if b >= 2:
                        pe.wait_ge(m_zero, 16 * (b - 1))
                    if b == 0:
                        pe.wait_ge(ld["mask"], 16)
                        pe.wait_ge(ld["identb"], 16)
                if n >= 2:
                    pe.wait_ge(max_done, n - 1)
                o = SQ[n % 2]
                if u < 8:
                    pe.matmul(o[:, :], identb[:], mask[:, :, :], start=True, stop=False, skip_group_check=True)
                    for h in range(4):
                        last = pe.matmul(o[:, h * P:(h + 1) * P], QT[i][:, 4 * u + h, 0:P], KT[i][:, u, 0:P],
                                         start=False, stop=True, skip_group_check=True)
                else:
                    h0 = 2 * (u - 8)
                    ov = o[:, :].rearrange("p (h k) -> p h k", h=2)
                    pe.matmul(ov[:, :, P:T], identb[:], mask[:, 0:2, :], start=True, stop=False,
                              skip_group_check=True)
                    for h in range(2):
                        last = pe.matmul(ov[:, h, :], QT[i][:, h0 + h, P:T], KT[i][:, h0 // REP, :],
                                         start=False, stop=True, skip_group_check=True)
                last.then_inc(sq_done, 1)

            def route(b, u):
                pe.wait_ge(mparts_done, b + 1)
                take("M0", (mrow_done, b + 1))
                for q in range(TC):
                    last = pe.transpose(M0b[0:3 * NH, q * P:(q + 1) * P],
                                        part_m[:, q, :, :].rearrange("p a h -> p (a h)"), identb[:])
                last.then_inc(mT_done, 1)

            TILES = ((0, 0), (0, 1), (1, 1))

            def at(b, u):
                i = b % 2
                g, (kc, q) = u // 3, TILES[u % 3]
                n = SU * b + u
                if u == 0:
                    pe.wait_ge(m_rows, 16 * (b + 1))
                    if b == 0:
                        pe.wait_ge(ones_rows, 32)
                if n >= 2:
                    pe.wait_ge(exp_done, n - 1)
                pe.matmul(ST[n % 2][:, :], KT[i][:, g, kc * P:(kc + 1) * P],
                          QT[i][:, REP * g:REP * (g + 1), q * P:(q + 1) * P], start=True, stop=True).then_inc(st_done, 1)

            def times_v(b, u):
                quad, k3 = divmod(u, 3)
                kc, q = TILES[k3]
                n = 2 * b + quad
                pe.wait_ge(exp_done, 12 * n + 10 + k3)
                if k3 != 1:
                    pe.wait_ge(causal_done, 8 * n + (7, 0, 8)[k3])
                if k3 == 0:
                    pe.wait_ge(v_done, b + 1)
                    if n >= 1:
                        pe.wait_ge(oT_done, n)
                for j in range(4):
                    g = 4 * quad + j
                    last = pe.matmul(PV[q][32 * j:32 * (j + 1), :], V[b % 2][:, kc, g, :],
                                     probs[:, (8 * b + g) % RING, k3, :],
                                     start=(k3 < 2), stop=(k3 != 1), skip_group_check=True)
                if k3 == 2:
                    last.then_inc(pv_done, 1)

            def turn(b, quad):
                pe.wait_ge(oT_done, 2 * b + quad + 1)
                for q in range(TC):
                    take(("M0", "M1")[q], (y_done, 4 * b + 2 * quad + q + 1))
                    for h in range(REP):
                        last = pe.transpose((M0, M1)[q][:, h * P:(h + 1) * P], oT[:, quad, q, h * P:(h + 1) * P], ident[:])
                    last.then_inc(ot_done, 1)

            def flip(src):
                for c in range(DC):
                    for q in range(TC):
                        last = pe.transpose(M0[:, c * T + q * P:c * T + (q + 1) * P], src[:, q, c * P:(c + 1) * P], ident[:])
                return last

            def times(lhsT, rhs):
                for q in range(TC):
                    for c in range(DC):
                        last = pe.matmul(M1[:, q * D:(q + 1) * D], lhsT[:, c, q * P:(q + 1) * P], rhs[:, c, :],
                                         start=(c == 0), stop=(c == DC - 1))
                return last

            def flip_y(b, u):
                pe.wait_ge(y_done, 4 * (b + 1))
                take("M0", (yT_done, b + 1))
                flip(y).then_inc(yt_done, 1)

            def wo(b, u):
                pe.wait_ge(yT_done, b + 1)
                if b == 0:
                    pe.wait_ge(ld["wo"], 16)
                take("M1", (res1_done, b + 1))
                times(yT, wo_s).then_inc(wo_done, 1)

            def flip_x1(b, u):
                pe.wait_ge(x1_done, b + 1)
                take("M0", (x1T_done, b + 1))
                flip(x1).then_inc(x1t_done, 1)

            def xm(b, u):
                pe.wait_ge(x1T_done, b + 1)
                pe.wait_ge(attT_done, b + 1)
                take("M1", (res2_done, b + 1))
                times(x1T, attT[b % 2]).then_inc(xm_done, 1)

            def flip_x2(b, u):
                pe.wait_ge(x2_done, b + 1)
                take("M0", (x2hi_done, b + 1), (x2lo_done, b + 1))
                flip(x2[:, b * TC:(b + 1) * TC, :]).then_inc(x2t_done, 1)

            def logits(b, u):
                pe.wait_ge(x2hi_done, b + 1)
                pe.wait_ge(x2lo_done, b + 1)
                if b == 0:
                    pe.wait_ge(wr_done, 2)
                take("M1", (lsub_done, b + 1))
                for q in range(TC):
                    tok = slice(b * T + q * P, b * T + (q + 1) * P)
                    n = 0
                    for xs, ws in ((x2T_hi, wr_hi), (x2T_hi, wr_lo), (x2T_lo, wr_hi)):
                        for c in range(DC):
                            last = pe.matmul(M1[:, q * E:(q + 1) * E], xs[:, c, tok], ws[:, c, :],
                                             start=(n == 0), stop=(n == 5))
                            n += 1
                last.then_inc(lg_done, 1)

            def turn_gate(b, u):
                pe.wait_ge(gparts_done, b + 1)
                take("M0", (gateT_done, b + 1))
                for q in range(TC):
                    last = pe.transpose(M0b[0:3 * NW, q * P:(q + 1) * P],
                                        part_g[:, q, :, :].rearrange("p a e -> p (a e)"), identb[:])
                last.then_inc(gT_done, 1)

            def xa_qk(b, u):
                pe.wait_ge(ld_ctxT[b], 16)
                if b == 0:
                    pe.wait_ge(ld["xaw"], 16)
                take("M0", (xqk_sb, 2 * (b + 1)))
                for j in range(2):
                    last = pe.matmul(M0[:, j * T:(j + 1) * T], xaw_s[:, j, :], ctxT_s[:, b % 2, :], start=True, stop=True)
                last.then_inc(xqk_done, 1)

            def xa_energy(b, u):
                pe.wait_ge(xqk_sb, 2 * (b + 1))
                take("M1", (xexp_done, 2 * (b + 1)))
                for r in range(TC):
                    last = pe.matmul(M1[:, r * T:(r + 1) * T], xaqk[:, 0, r * P:(r + 1) * P], xaqk[:, 1, :],
                                     start=True, stop=True)
                last.then_inc(xen_done, 1)

            def xa_flip(b, u):
                pe.wait_ge(xatt_done, 2 * (b + 1))
                take("M0", (attT_done, b + 1))
                flip(xae).then_inc(xat_done, 1)

            def open_sums(h, u):
                if h == 0:
                    pe.wait_ge(exp_done, SU * B)
                else:
                    pe.wait_ge(hid_done, EARLY)
                for k in range(2 * h, 2 * h + 2):
                    pe.matmul(bank[k][:, :], zero[:, 0:P], zero[:, :], start=True, stop=False, skip_group_check=True)

            def gate_up(n, j):
                c, half = STEP[n]
                fn = FN[c]
                tok = slice(half * HALF, (half + 1) * HALF)
                if j == 0:
                    if half == 0:
                        pe.wait_ge(whi_done, c + 1)
                        pe.wait_ge(wlo_done, c + 1)
                    if n == 0:
                        pe.wait_ge(oT_done, 2 * B)
                    if n == 1:
                        pe.wait_ge(max_done, SU * B)
                    if n == EARLY:
                        pe.wait_ge(x2hi_done, B)
                        pe.wait_ge(x2lo_done, B)
                    if n == EARLY + 1:
                        for name in readers:
                            take(name)
                    if n >= 2:
                        pe.wait_ge(hid_done, n - 1)
                k = 0
                for ws, xs in ((w_hi, x2T_hi), (w_hi, x2T_lo), (w_lo, x2T_hi)):
                    for d in range(DC):
                        col = (j * DC + d) * P
                        last = pe.matmul(GU[n][j][0:fn, :], ws[c % WRING][:, col:col + fn], xs[:, d, tok],
                                         start=(k == 0), stop=(k == 5))
                        k += 1
                last.then_inc(gu_done, 1)

            def spread(n, u):
                c, half = STEP[n]
                fn = FN[c]
                if n == 0:
                    pe.wait_ge(ld["sel"], 16)
                    pe.wait_ge(gateT_done, B // 2)
                if n == EARLY:
                    pe.wait_ge(gateT_done, B)
                pe.wait_ge(silu_done, n + 1)
                pe.matmul(GU[n][0][0:fn, :], sel[:, c * P:c * P + fn],
                          gateT[:, half * HALF:(half + 1) * HALF], start=True, stop=True).then_inc(spread_done, 1)

            def down(n, u):
                c, half = STEP[n]
                fn = FN[c]
                pe.wait_ge(hhi_done, n + 1)
                for hs, ws in ((h_hi, w_hi), (h_hi, w_lo), (h_lo, w_hi)):
                    if hs is h_lo:
                        pe.wait_ge(hlo_done, n + 1)
                    for t4 in range(HALF // P):
                        t = half * (HALF // P) + t4
                        last = pe.matmul(bank[t // 2][:, (t % 2) * D:(t % 2 + 1) * D], hs[n % 2][0:fn, t4 * P:(t4 + 1) * P],
                                         ws[c % WRING][0:fn, GUW:WW], start=False, stop=False, skip_group_check=True)
                        if hs is h_lo and c == NCH - 1 and t4 == 1:
                            last.then_inc(sums_done, 1)
                last.then_inc(down_done, 1)

            write({"proj": proj, "turn_v": turn_v, "mx": mx, "route": route, "at": at, "times_v": times_v, "turn": turn,
                   "flip_y": flip_y, "wo": wo, "flip_x1": flip_x1, "xm": xm, "flip_x2": flip_x2, "logits": logits,
                   "turn_gate": turn_gate, "xa_qk": xa_qk, "xa_energy": xa_energy, "xa_flip": xa_flip,
                   "open": open_sums, "gate_up": gate_up, "spread": spread, "down": down})

        @block.scalar
        def _(act):
            def copy(dst, src):
                return nc.scalar.activation(dst, src, ACT.Copy)

            def proj(b, u):
                act.wait_ge(kv_done, b + 1)
                if b >= 2:
                    act.wait_ge(qk_rows[b % 2], ROWS * (b // 2))
                copy(part_k[b % 2][64:, 0, :], M1[64:, 0:T]).then_inc(k_parts[0], 1)
                if b >= 1:
                    act.wait_ge(vt_done, b)
                copy(vT[:], M1[0:64, 0:T]).then_inc(vT_done, 1)
                act.wait_ge(q_done, b + 1)
                copy(part_q[b % 2][:, 0, :], M0[:, :]).then_inc(q_parts[0], 1)

            def turn_v(b, u):
                act.wait_ge(vt_done, b + 1)
                if b == 0:
                    act.wait_ge(init_v, 4)
                if b >= 2:
                    act.wait_ge(pv_done, 2 * (b - 1))
                copy(V[b % 2][:, :, :, 0:HD],
                     M1[:, 0:TC * 64].rearrange("p (t g d) -> p t g d", t=TC, g=NKV)).then_inc(v_done, 1)

            def route(b, u):
                act.wait_ge(mT_done, b + 1)
                if b >= 1:
                    act.wait_ge(m_rows, 16 * b)
                copy(mrow[:], M0b[0:3 * NH, 0:T]).then_inc(mrow_done, 1)

            def at(b, u):
                g, k = u // 3, u % 3
                n = SU * b + u
                slot = 8 * b + g
                if k == 0 and slot >= RING:
                    act.wait_ge(pv_done, (slot - RING) // 4 + 1)
                act.wait_ge(st_done, n + 1)
                nc.scalar.activation(probs[:, slot % RING, k, :], ST[n % 2][:, :], ACT.Exp,
                                     scale=SCALE).then_inc(exp_done, 1)

            def take_out(b, quad):
                act.wait_ge(pv_done, 2 * b + quad + 1)
                if b >= 1:
                    act.wait_ge(ot_done, 4 * b - 2 + 2 * quad)
                copy(oT[:, quad, 0, :], PV[0][:, :])
                copy(oT[:, quad, 1, :], PV[1][:, :]).then_inc(oT_done, 1)

            def flip_y(b, u):
                act.wait_ge(yt_done, b + 1)
                if b >= 1:
                    act.wait_ge(wo_done, b)
                copy(yT[:, :, :].rearrange("p c t -> p (c t)"), M0[:, :]).then_inc(yT_done, 1)

            def flip_x1(b, u):
                act.wait_ge(x1t_done, b + 1)
                if b >= 1:
                    act.wait_ge(xm_done, b)
                copy(x1T[:, :, :].rearrange("p c t -> p (c t)"), M0[:, :]).then_inc(x1T_done, 1)

            def flip_x2(b, u):
                act.wait_ge(x2t_done, b + 1)
                copy(x2T_hi[:, :, b * T:(b + 1) * T], M0[:, :].rearrange("p (c t) -> p c t", c=DC)).then_inc(x2hi_done, 1)

            def logits(b, u):
                act.wait_ge(lsub_done, b + 1)
                nc.scalar.activation(lexp[:], lsub[:], ACT.Exp).then_inc(lexp_done, 1)

            def turn_gate(b, u):
                act.wait_ge(gT_done, b + 1)
                copy(gateT[:, b * T:(b + 1) * T], M0b[0:3 * NW, 0:T]).then_inc(gateT_done, 1)

            def xa_energy(b, u):
                act.wait_ge(xmax_done, b + 1)
                if b >= 1:
                    act.wait_ge(xat_done, b)
                for r in range(TC):
                    nc.scalar.activation(xae[:, r, :], M1[:, r * T:(r + 1) * T], ACT.Exp, bias=xam[:, r:r + 1],
                                         accum_out=xal[:, r:r + 1]).then_inc(xexp_done, 1)

            def xa_flip(b, u):
                act.wait_ge(xat_done, b + 1)
                if b >= 2:
                    act.wait_ge(xm_done, b - 1)
                copy(attT[b % 2][:, :, :].rearrange("p c t -> p (c t)"), M0[:, :]).then_inc(attT_done, 1)

            def silu(n, u):
                fn = FN[STEP[n][0]]
                act.wait_ge(gu_done, 2 * n + 1)
                if n == 0:
                    act.wait_ge(pv_done, 2 * B)
                if n >= 2:
                    act.wait_ge(prod_done, n - 1)
                nc.scalar.activation(sg[n % 2][0:fn, :], GU[n][0][0:fn, :], ACT.Silu).then_inc(silu_done, 1)

            def hidden_hi(n, u):
                fn = FN[STEP[n][0]]
                act.wait_ge(hid_done, n + 1)
                if n >= 2:
                    act.wait_ge(down_done, n - 1)
                copy(h_hi[n % 2][0:fn, :], hid[n % 2][0:fn, :]).then_inc(hhi_done, 1)

            write({"PROJ": proj, "TURN_V": turn_v, "ROUTE": route, "at": at, "TIMES_V": take_out, "FLIP_Y": flip_y,
                   "FLIP_X1": flip_x1, "FLIP_X2": flip_x2, "LOGITS": logits, "TURN_GATE": turn_gate,
                   "XA_ENERGY": xa_energy, "XA_FLIP": xa_flip, "SILU": silu, "HID_HI": hidden_hi})

        @block.vector
        def _(v):
            ve = nc.vector
            own = [0]

            def step(ins):
                own[0] += 1
                return ins.then_inc(dve, 1)

            def settle():
                v.wait_ge(dve, own[0])

            ve.memset(zero[:], 0.0).then_inc(init_v, 1)
            ve.memset(QT[0][:, :, :].rearrange("p a b -> p (a b)").bitcast(F32), 0.0).then_inc(init_qt, 1)
            ve.memset(mhalf[:], -0.5).then_inc(init_v, 1)
            for i in range(2):
                step(ve.memset(V[i][:], 0.0))
            settle()
            for i in range(2):
                ve.memset(V[i][:, :, :, HD:HD + 1], 1.0).then_inc(init_v, 1)
            ve.memset(gatew[:, :, E:NW], 1.0).then_inc(init_v, 1)

            def proj(b, u):
                def split(rest, psum, part, done):
                    v.wait_ge(done[0], b + 1)
                    step(ve.tensor_tensor(rest, psum, part(0), ALU.subtract))
                    settle()
                    ve.tensor_copy(part(1), rest).then_inc(done[1], 1)
                    v.wait_ge(done[1], b + 1)
                    ve.tensor_tensor(part(2), rest, part(1), ALU.subtract).then_inc(done[2], 1)

                v.wait_ge(vT_done, b + 1)
                if b >= 1:
                    v.wait_ge(k_parts[2], b)
                split(rest_k[64:, :], M1[64:, 0:T], lambda p: part_k[b % 2][64:, p, :], k_parts)
                split(rest_q, M0[:, :], lambda p: part_q[b % 2][:, p, :], q_parts)
                v.wait_ge(q_parts[2], b + 1)

            def mx(b, u):
                n = SU * b + u
                v.wait_ge(sq_done, n + 1)
                if u < 8:
                    o, src = negmax[:, 0, 4 * u:4 * u + 4], SQ[n % 2][:, :].rearrange("p (h k) -> p h k", h=4)
                else:
                    h0 = 2 * (u - 8)
                    o, src = negmax[:, 1, h0:h0 + 2], SQ[n % 2][:, :].rearrange("p (h k) -> p h k", h=2)
                ve.tensor_reduce(o, src, AX_X, ALU.max, negate=True).then_inc(max_done, 1)

            def max_parts(b, u):
                v.wait_ge(max_done, SU * (b + 1))
                if b >= 1:
                    v.wait_ge(mT_done, b)
                    v.wait_ge(mparts_done, b)
                step(ve.tensor_copy(part_m[:, :, 0, :], negmax[:]))
                settle()
                step(ve.tensor_tensor(rest_m[:], negmax[:], part_m[:, :, 0, :], ALU.subtract))
                settle()
                step(ve.tensor_copy(part_m[:, :, 1, :], rest_m[:]))
                settle()
                ve.tensor_tensor(part_m[:, :, 2, :], rest_m[:], part_m[:, :, 1, :], ALU.subtract).then_inc(mparts_done, 1)

            def normalise(b, quad):
                for q in range(TC):
                    n = 4 * b + 2 * quad + q
                    v.wait_ge(ot_done, n + 1)
                    m = (M0, M1)[q][:, :].rearrange("p (h j c) -> p h j c", h=REP, j=4)
                    if n:
                        v.wait_ge(y_done, n)
                    step(ve.reciprocal(rden[:, :].rearrange("p (h j) -> p h j", h=REP), m[:, :, :, HD]))
                    settle()
                    if b >= 1:
                        v.wait_ge(yt_done, b)
                    o = y[:, q, quad * P:(quad + 1) * P].rearrange("p (j h d) -> p h j d", j=4, h=REP)
                    den = rden[:, :].rearrange("p (h j o) -> p h j o", h=REP, o=1).to_broadcast([P, REP, 4, HD])
                    ve.tensor_tensor(o, m[:, :, :, 0:HD], den, ALU.mult).then_inc(y_done, 1)

            norms, norm_in = [0], [0, 0]

            def statistics(src, k):
                tiles = range(k * TC, (k + 1) * TC)
                for q in tiles:
                    step(ve.bn_stats(stat[:, q, :], src[:, q, :]))
                settle()
                for q in tiles:
                    step(ve.bn_aggr(mv[:, q, :], stat[:, q, :]))
                settle()
                mine = slice(k * TC, (k + 1) * TC)
                ve.tensor_scalar(veps[:, mine], mv[:, mine, 1], EPS, None, ALU.add).then_inc(var_done, 1)
                norms[0] += 1
                norm_in[k] = norms[0]

            def apply_norm(dst, src, k, done, value):
                v.wait_ge(rstd_done, norm_in[k])
                for q in range(TC):
                    p = k * TC + q
                    last = ve.tensor_scalar(dst[:, q, :], src[:, p, :], mv[:, p, 0:1], rstd[:, p:p + 1],
                                            ALU.subtract, ALU.mult)
                    if q < TC - 1:
                        step(last)
                last.then_inc(done, 1)
                settle()
                v.wait_ge(done, value)

            def residual(dst, m, x, done):
                ve.tensor_tensor(dst[:, :, :].rearrange("p q d -> p (q d)"), m,
                                 x.rearrange("p q d -> p (q d)"), ALU.add).then_inc(done, 1)

            def norm1(b, part):
                if part == 0:
                    if b == 0:
                        v.wait_ge(ld["x"], 16)
                    v.wait_ge(wo_done, b + 1)
                    residual(res, M1[:, :], x_s[:, b * TC:(b + 1) * TC, :], res1_done)
                    v.wait_ge(res1_done, b + 1)
                    statistics(res, 0)
                else:
                    if b >= 1:
                        v.wait_ge(x1t_done, b)
                    apply_norm(x1, res, 0, x1_done, b + 1)

            def norm2(b, part):
                if part == 0:
                    v.wait_ge(xm_done, b + 1)
                    residual(res, M1[:, :], x1[:, :, :], res2_done)
                    v.wait_ge(res2_done, b + 1)
                    statistics(res, 0)
                else:
                    apply_norm(x2[:, b * TC:(b + 1) * TC, :], res, 0, x2_done, b + 1)

            def flip_x2(b, u):
                v.wait_ge(x2hi_done, b + 1)
                ve.tensor_tensor(x2T_lo[:, :, b * T:(b + 1) * T], M0[:, :].rearrange("p (c t) -> p c t", c=DC),
                                 x2T_hi[:, :, b * T:(b + 1) * T].bitcast(F32), ALU.subtract).then_inc(x2lo_done, 1)

            def per_tile(a):
                return a[:, :].rearrange("p (q o) -> p q o", o=1).to_broadcast([P, TC, E])

            def router(b, u):
                v.wait_ge(lg_done, b + 1)
                logits = M1[:, 0:TC * E].rearrange("p (q e) -> p q e", q=TC)
                step(ve.tensor_reduce(lmax[:], logits, AX_X, ALU.max))
                settle()
                ve.tensor_tensor(lsub[:], logits, per_tile(lmax), ALU.subtract).then_inc(lsub_done, 1)

            def score_ranks(b, u):
                v.wait_ge(lexp_done, b + 1)
                step(ve.tensor_reduce(lsum[:], lexp[:], AX_X, ALU.add))
                settle()
                step(ve.reciprocal(lsum[:], lsum[:]))
                settle()
                step(ve.tensor_tensor(score[:], lexp[:], per_tile(lsum), ALU.mult))
                settle()
                if b == 0:
                    v.wait_ge(ld["lower"], 16)
                for q in range(TC):
                    mine = score[:, q, :].rearrange("p (e o) -> p e o", o=1).to_broadcast([P, E, E])
                    other = score[:, q, :].rearrange("p (o j) -> p o j", o=1).to_broadcast([P, E, E])
                    step(ve.tensor_tensor(above[:, q], other, mine, ALU.is_gt))
                    step(ve.tensor_tensor(equal[:, q], other, mine, ALU.is_equal))
                settle()

            def gates(b, u):
                for q in range(TC):
                    step(ve.tensor_tensor(equal[:, q], equal[:, q], lower[:], ALU.mult))
                settle()
                step(ve.tensor_tensor(above[:], above[:], equal[:], ALU.add))
                settle()
                step(ve.tensor_reduce(rank[:], above[:], AX_X, ALU.add))
                settle()
                step(ve.scalar_tensor_tensor(gatew[:, :, 0:E], rank[:], 2.0, score[:], ALU.is_lt, ALU.mult))
                settle()
                if b >= 1:
                    v.wait_ge(gT_done, b)
                    v.wait_ge(gparts_done, b)
                if b == 0:
                    v.wait_ge(init_v, 5)
                step(ve.tensor_copy(part_g[:, :, 0, :], gatew[:]))
                settle()
                step(ve.tensor_tensor(rest_g[:], gatew[:], part_g[:, :, 0, :], ALU.subtract))
                settle()
                step(ve.tensor_copy(part_g[:, :, 1, :], rest_g[:]))
                settle()
                ve.tensor_tensor(part_g[:, :, 2, :], rest_g[:], part_g[:, :, 1, :], ALU.subtract).then_inc(gparts_done, 1)

            def xa_qk(b, u):
                if b == 0:
                    v.wait_ge(ld["wr"], 16)
                    ve.tensor_copy(wr_hi[:], wr_s[:]).then_inc(wr_done, 1)
                    v.wait_ge(wr_done, 1)
                    ve.tensor_tensor(wr_lo[:], wr_s[:], wr_hi[:].bitcast(F32), ALU.subtract).then_inc(wr_done, 1)
                    v.wait_ge(ld["xab"], 16)
                v.wait_ge(xqk_done, b + 1)
                if b >= 1:
                    v.wait_ge(xen_done, b)
                for j in range(2):
                    ve.tensor_scalar(xaqk[:, j, :], M0[:, j * T:(j + 1) * T], xab_s[:, j:j + 1], None,
                                     ALU.add).then_inc(xqk_sb, 1)

            def xa_energy(b, u):
                v.wait_ge(xen_done, b + 1)
                if b >= 1:
                    v.wait_ge(xexp_done, 2 * b)
                    v.wait_ge(xatt_done, 2 * b)
                ve.tensor_reduce(xam[:], M1[:, :].rearrange("p (r k) -> p r k", r=TC), AX_X, ALU.max,
                                 negate=True).then_inc(xmax_done, 1)

            def xa_scale(b, u):
                v.wait_ge(xexp_done, 2 * (b + 1))
                step(ve.reciprocal(xar[:], xal[:]))
                settle()
                for r in range(TC):
                    ve.tensor_scalar(xae[:, r, :], xae[:, r, :], xar[:, r:r + 1], None, ALU.mult).then_inc(xatt_done, 1)

            def weights_hi(c, u):
                v.wait_ge(ld_w[c % 2], 16 * (c // 2 + 1))
                if c == WOWN:
                    v.wait_ge(pv_done, 2 * B)
                if c >= WRING:
                    v.wait_ge(down_done, STEP.index((c - WRING, NHALF - 1)) + 1)
                ve.tensor_copy(w_hi[c % WRING][:], w_in[:, c % 2]).then_inc(whi_done, 1)

            def product(n, u):
                fn = FN[STEP[n][0]]
                v.wait_ge(silu_done, n + 1)
                v.wait_ge(gu_done, 2 * (n + 1))
                if n >= 2:
                    v.wait_ge(hid_done, n - 1)
                ve.tensor_tensor(gu[n % 2][0:fn, :], GU[n][1][0:fn, :], sg[n % 2][0:fn, :], ALU.mult).then_inc(prod_done, 1)

            def hidden(n, u):
                fn = FN[STEP[n][0]]
                v.wait_ge(prod_done, n + 1)
                v.wait_ge(spread_done, n + 1)
                if n >= 2:
                    v.wait_ge(hhi_done, n - 1)
                    v.wait_ge(hlo_done, n - 1)
                ve.tensor_tensor(hid[n % 2][0:fn, :], GU[n][0][0:fn, :], gu[n % 2][0:fn, :], ALU.mult).then_inc(hid_done, 1)

            def last_norm(b, part):
                h, k = divmod(b, 2)
                tiles = slice(k * TC, (k + 1) * TC)
                if part == 0:
                    if k == 0:
                        v.wait_ge(sums_done, h + 1)
                    else:
                        v.wait_ge(down_done, STEP.index((NCH - 1, h)) + 1)
                    step(ve.tensor_tensor(res_l[:, tiles, :].rearrange("p q d -> p (q d)"), bank[b][:, :],
                                          x2[:, b * TC:(b + 1) * TC, :].rearrange("p q d -> p (q d)"), ALU.add))
                    settle()
                    statistics(res_l, k)
                else:
                    apply_norm(x_s[:, b * TC:(b + 1) * TC, :], res_l, k, out_done, b + 1)

            write({"PROJ": proj, "mx": mx, "MAX_PARTS": max_parts, "TURN": normalise, "NORM1": norm1, "NORM2": norm2,
                   "FLIP_X2": flip_x2, "LOGITS": router, "SCORES": score_ranks, "GATES": gates, "XA_QK": xa_qk,
                   "XA_ENERGY": xa_energy, "XA_SCALE": xa_scale,
                   "WEIGHTS": weights_hi, "PROD": product, "HID": hidden, "LAST_NORM": last_norm})

        @block.gpsimd
        def _(pool):
            gp = nc.gpsimd
            gp.memset(ones[:], 1.0).then_inc(init_p, 1)
            for tile in (KT[0], KT[1], QT[1]):
                gp.memset(tile[:, :, :].rearrange("p a b -> p (a b)").bitcast(F32), 0.0).then_inc(init_p, 1)
            norms = [0]

            def rsqrt(k):
                if norms[0] == 0:
                    pool.wait_ge(init_v, 2)
                norms[0] += 1
                pool.wait_ge(var_done, norms[0])
                mine = slice(k * TC, (k + 1) * TC)
                gp.tensor_tensor(rstd[:, mine], veps[:, mine], mhalf[:, mine], ALU.pow).then_inc(rstd_done, 1)

            def at(b, u):
                if u % 3 == 1:
                    return
                pool.wait_ge(exp_done, SU * b + u + 1)
                t = probs[:, (8 * b + u // 3) % RING, u % 3, :].rearrange("p (h q) -> p h q", h=REP)
                gp.affine_select(out=t, in_=t, compare_op=ALU.is_ge, fill=0.0, base=0,
                                 pattern=[[0, REP], [1, P]], channel_multiplier=-1).then_inc(causal_done, 1)

            def norm(b, part):
                if part == 0:
                    rsqrt(0)

            def weights_lo(c, u):
                pool.wait_ge(whi_done, c + 1)
                gp.tensor_tensor(w_lo[c % WRING][:], w_in[:, c % 2], w_hi[c % WRING][:].bitcast(F32),
                                 ALU.subtract).then_inc(wlo_done, 1)

            def hidden_lo(n, u):
                fn = FN[STEP[n][0]]
                pool.wait_ge(hhi_done, n + 1)
                if n >= 2:
                    pool.wait_ge(down_done, n - 1)
                gp.tensor_tensor(h_lo[n % 2][0:fn, :], hid[n % 2][0:fn, :], h_hi[n % 2][0:fn, :].bitcast(F32),
                                 ALU.subtract).then_inc(hlo_done, 1)

            def last_norm(b, part):
                if part == 0:
                    rsqrt(b % 2)

            write({"at": at, "NORM1": norm, "NORM2": norm, "WEIGHTS": weights_lo, "HID_LO": hidden_lo,
                   "LAST_NORM": last_norm})


def constants():
    bf = np.dtype("bfloat16")
    ident = np.eye(P, dtype=np.float32)
    later = np.arange(P)[None, :] > np.arange(P)[:, None]
    mask = np.repeat(np.where(later, MASKED, 0.0)[:, None, :], REP, axis=1).astype(bf)
    sel = np.zeros((3, NW, NCH * P), np.float32)
    for f in range(F):
        sel[:, min(f // FE, E), f] = 1.0
    lower = np.tile(np.tril(np.ones((E, E), np.float32), -1), (P, 1, 1))
    return {"c_ident": ident, "c_identb": ident.astype(bf), "c_mask": mask,
            "c_sel": sel.reshape(3 * NW, NCH * P).astype(bf), "c_lower": lower}


def rows(a, chunks):
    return np.ascontiguousarray(a.reshape(chunks, P, -1).transpose(1, 0, 2))


def kernel(**inputs):
    from concourse import bacc
    from concourse.bass_utils import run_bass_kernel_spmd

    a = {k: np.asarray(v) for k, v in inputs.items()}
    x = a["x"].reshape(B * T, D)
    wq = a["L0_attn_wq"].reshape(D, NH // 2, 2, HD).transpose(0, 2, 3, 1).reshape(D, NH * HD)
    wk = a["L0_attn_wk"].reshape(D, NKV, HD).transpose(0, 2, 1).reshape(D, NKV * HD)
    gate, up = (np.concatenate([a[n].reshape(E * FE, D), a[m]]).T
                for n, m in (("L0_ffn_Wg", "L0_ffn_Wsg"), ("L0_ffn_Wu", "L0_ffn_Wsu")))
    down = np.concatenate([a["L0_ffn_Wd"].transpose(0, 2, 1).reshape(E * FE, D), a["L0_ffn_Wsd"].T])
    w_ffn = np.zeros((NCH, P, WW), np.float32)
    for c, fn in enumerate(FN):
        f = slice(c * P, c * P + fn)
        for j, w in enumerate((gate, up)):
            for d in range(DC):
                w_ffn[c, :, (j * DC + d) * P:(j * DC + d) * P + fn] = w[d * P:(d + 1) * P, f]
        w_ffn[c, :fn, GUW:] = down[f]
    arrays = {
        "x_tok": rows(x, B * TC),
        "x_T": rows(np.ascontiguousarray(x.T), DC),
        "ctx_T": np.ascontiguousarray(a["ctx_1024"].reshape(B * T, CTX).T),
        "w_qkv": rows(np.concatenate([wq, a["L0_attn_wv"], wk], axis=1), DC),
        "w_o": rows(a["L0_attn_wo"], DC),
        "xa_w": np.ascontiguousarray(np.stack([a["L0_xattn_Wq"].T, a["L0_xattn_Wk"].T], axis=1)),
        "xa_b": np.ascontiguousarray(np.stack([a["L0_xattn_bq"], a["L0_xattn_bk"]], axis=1)),
        "w_r": rows(np.ascontiguousarray(a["L0_ffn_Wr"].T), DC),
        "w_ffn": w_ffn,
        **constants(),
    }
    nc = bacc.Bacc("TRN2", target_bir_lowering=False, num_devices=1)
    args = [nc.dram_tensor(n, v.shape, mybir.dt.from_np(v.dtype), kind="ExternalInput").ap() for n, v in arrays.items()]
    out = nc.dram_tensor("out", (B, P, TC, D), F32, kind="ExternalOutput").ap()
    build_layer(nc, *args, out)
    r = run_bass_kernel_spmd(nc, [arrays], core_ids=[0])
    return np.asarray(r.results[0]["out"]).transpose(0, 2, 1, 3).reshape(B, T, D)
```
